# Optimizing a Trainium2 kernel written in Bass

```python
import numpy as np
import jax
import jax.numpy as jnp

def _softmax(x, axis=-1):
    return jax.nn.softmax(x, axis=axis)

def _gelu(x):
    return jax.nn.gelu(x, approximate=True)

def _silu(x):
    return jax.nn.silu(x)

def _sigmoid(x):
    return jax.nn.sigmoid(x)

def _layernorm(x, axis=-1, eps=1e-05):
    m = jnp.mean(x, axis=axis, keepdims=True)
    v = jnp.var(x, axis=axis, keepdims=True)
    return (x - m) / jnp.sqrt(v + eps)

def _scatter_add(tgt, idx, src, axis=0):
    return tgt.at[idx].add(src)

def _segment_sum(src, seg, n):
    return jax.ops.segment_sum(src, seg, n)
kernel_name = 'mk_xattn_seq_d1_seqx_r2_13e2b8'

def setup_inputs(seed: int=0):
    np.random.seed(seed)
    _w = jnp.asarray

    def _rec_inputs():
        import jax
        import jax.numpy as jnp
        _rk = jax.random.key(seed)
        x = -0.0002928 + 1 * jax.random.normal(jax.random.fold_in(_rk, 1), (8, 1024, 512), jnp.float32)
        _lenS = 1024 - jax.random.randint(jax.random.fold_in(_rk, 7), (8,), 0, max(1, 1024 // 4) + 1, jnp.int32)
        _lenS2 = 64 - jax.random.randint(jax.random.fold_in(_rk, 8), (8,), 0, max(1, 64 // 4) + 1, jnp.int32)
        _ctx_1024P = jax.random.normal(jax.random.fold_in(_rk, 11), (8, 16, 512), jnp.float32)
        _ctx_1024c = jax.random.dirichlet(jax.random.fold_in(_rk, 511), 0.3 * jnp.ones((16,), jnp.float32), (8, 64))
        _ctx_1024t = jnp.einsum('bsk,bkd->bsd', _ctx_1024c, _ctx_1024P)
        _ctx_1024t = _ctx_1024t * jax.lax.rsqrt(jnp.mean(jnp.square(_ctx_1024t)) + 1e-12) * 0.953939
        ctx_1024 = -1.39393e-06 + 0.999914 * (_ctx_1024t + 0.3 * jax.random.normal(jax.random.fold_in(_rk, 611), (8, 64, 512), jnp.float32))
        return (x, ctx_1024)
    x, ctx_1024 = _rec_inputs()

    def _L0_xattn_setup():
        import jax, jax.numpy as jnp
        import numpy as np
        D_MODEL = 512
        NUM_HEADS = 16
        D_K = D_MODEL // NUM_HEADS
        LN_EPS = 1e-05
        key = jax.random.key(seed)
        ks = jax.random.split(key, 9)
        B, S = (2, 1024)
        scale = 1.0 / np.sqrt(D_MODEL)
        return {'query': jax.random.normal(ks[0], (B, S, D_MODEL), jnp.float32), 'key': jax.random.normal(ks[1], (B, S, D_MODEL), jnp.float32), 'value': jax.random.normal(ks[2], (B, S, D_MODEL), jnp.float32), 'w_q': jax.random.normal(ks[3], (D_MODEL, D_MODEL), jnp.float32) * scale, 'w_k': jax.random.normal(ks[4], (D_MODEL, D_MODEL), jnp.float32) * scale, 'w_v': jax.random.normal(ks[5], (D_MODEL, D_MODEL), jnp.float32) * scale, 'w_o': jax.random.normal(ks[6], (D_MODEL, D_MODEL), jnp.float32) * scale, 'b_o': jnp.zeros((D_MODEL,), jnp.float32), 'ln_gamma': jnp.ones((D_MODEL,), jnp.float32), 'ln_beta': jnp.zeros((D_MODEL,), jnp.float32)}
    _L0_xattn_all = _L0_xattn_setup()
    _L0_xattn_in = {k: v for k, v in _L0_xattn_all.items() if k in ('w_q', 'w_k', 'w_v', 'w_o', 'b_o', 'ln_gamma', 'ln_beta')}
    del _L0_xattn_all
    return {'x': x, 'ctx_1024': ctx_1024, 'L0_xattn_w_q': _L0_xattn_in['w_q'], 'L0_xattn_w_k': _L0_xattn_in['w_k'], 'L0_xattn_w_v': _L0_xattn_in['w_v'], 'L0_xattn_w_o': _L0_xattn_in['w_o'], 'L0_xattn_b_o': _L0_xattn_in['b_o'], 'L0_xattn_ln_gamma': _L0_xattn_in['ln_gamma'], 'L0_xattn_ln_beta': _L0_xattn_in['ln_beta']}

def reference(x, ctx_1024, L0_xattn_w_q, L0_xattn_w_k, L0_xattn_w_v, L0_xattn_w_o, L0_xattn_b_o, L0_xattn_ln_gamma, L0_xattn_ln_beta):
    import jax
    import jax.numpy as jnp

    def _L0_xattn_ref(query, key, value, w_q, w_k, w_v, w_o, b_o, ln_gamma, ln_beta):
        import jax, jax.numpy as jnp
        import numpy as np
        D_MODEL = 512
        NUM_HEADS = 16
        D_K = D_MODEL // NUM_HEADS
        LN_EPS = 1e-05
        B, S, _ = query.shape
        Q = (query @ w_q.T).reshape(B, S, NUM_HEADS, D_K).transpose(0, 2, 1, 3)
        K = (key @ w_k.T).reshape(B, -1, NUM_HEADS, D_K).transpose(0, 2, 1, 3)
        V = (value @ w_v.T).reshape(B, -1, NUM_HEADS, D_K).transpose(0, 2, 1, 3)
        scores = jnp.einsum('bhqd,bhkd->bhqk', Q, K) / np.sqrt(D_K)
        attn = jax.nn.softmax(scores, axis=-1)
        ctx = jnp.einsum('bhqk,bhkd->bhqd', attn, V)
        ctx = ctx.transpose(0, 2, 1, 3).reshape(B, S, D_MODEL)
        out = ctx @ w_o.T + b_o
        x = out + query
        mu = jnp.mean(x, axis=-1, keepdims=True)
        var = jnp.mean(jnp.square(x - mu), axis=-1, keepdims=True)
        return (x - mu) * jax.lax.rsqrt(var + LN_EPS) * ln_gamma + ln_beta
    x = _L0_xattn_ref(x, ctx_1024, ctx_1024, L0_xattn_w_q, L0_xattn_w_k, L0_xattn_w_v, L0_xattn_w_o, L0_xattn_b_o, L0_xattn_ln_gamma, L0_xattn_ln_beta)
    return x

_drawn_inputs = setup_inputs


def setup_inputs(seed=0):
    import zlib

    import numpy as np

    out = dict(_drawn_inputs(seed))
    spreads = {'L0_xattn_b_o': (0.0, 0.1),
     'L0_xattn_ln_gamma': (1.0, 0.2),
     'L0_xattn_ln_beta': (0.0, 0.1)}
    factors = {}
    for name, (base, spread) in spreads.items():
        noise = np.random.default_rng([zlib.crc32(name.encode()), seed]).standard_normal(out[name].shape)
        drawn = base * np.exp(spread * noise) if base else spread * noise
        out[name] = jnp.asarray(drawn.astype(out[name].dtype))
    for name, factor in factors.items():
        out[name] = (out[name] * factor).astype(out[name].dtype)
    return out
```

```python
from collections import namedtuple
from contextlib import ExitStack

import concourse.bass as bass
from concourse import mybir

Step = namedtuple("Step", "c odd batch split stage1 stage2 output next_keys next_values")


def cross_attention_kernel(nc, xT, x, ctxT, wqT, wkT, wvT, woT, b_o, gamma, beta, out):
    fp32, fp32r = mybir.dt.float32, mybir.dt.float32r
    ALU, ACT, AX = mybir.AluOpType, mybir.ActivationFunctionType, mybir.AxisListType

    P = 128
    DM, ROWS = xT.shape
    CTX_ROWS = ctxT.shape[1]
    BATCHES, HEADS = 8, 16
    KEYS = CTX_ROWS // BATCHES
    DK = DM // HEADS
    KT = DM // P
    CHUNK = 512
    CHUNKS = ROWS // CHUNK
    G = KT
    HG = HEADS // G
    PAIRS = HG // 2
    UNITS = 2
    UH = UNITS * HG
    TILES = CHUNKS * G
    SCALE = float(DK) ** -0.5
    EPS = 1e-5
    assert CHUNKS == 2 * BATCHES and G == CHUNK // P and 2 * KEYS == P and KT * P == DM

    def step_of(c, odd, batch, whole=False):
        if whole:
            return Step(c, odd, batch, True, True, True, True, not odd, odd)
        return Step(c, odd, batch, c + 2 < CHUNKS, 0 <= c + 1 < CHUNKS, 0 <= c < CHUNKS,
                    0 <= c - 1, not odd and batch + 1 < BATCHES, odd and 0 <= batch < BATCHES)

    def all_steps(eng, slot):
        for c in range(-2, 3):
            for g in range(G):
                slot(step_of(c, c % 2, (c + 1) // 2), g)
        with eng.Fori(1, BATCHES - 2) as i:
            for odd in (1, 0):
                for g in range(G):
                    slot(step_of(2 * i + (2 - odd), odd, i + 1, whole=True), g)
        for c in range(CHUNKS - 3, CHUNKS + 1):
            for g in range(G):
                slot(step_of(c, c % 2, (c + 1) // 2), g)

    def wait(eng, sem, value):
        if not isinstance(value, int) or value > 0:
            eng.wait_ge(sem, value)

    xT_v = xT.rearrange("(k p) n -> k p n", p=P)
    ctxT_v, wqT_v, wkT_v, wvT_v, woT_v = (
        a.rearrange("(k p) n -> k p n", p=P) for a in (ctxT, wqT, wkT, wvT, woT))

    with ExitStack() as ctx:
        def sb(name, shape, dt, stack=ctx):
            return stack.enter_context(nc.sbuf_tensor(name, shape, dt))

        def sem(name):
            return ctx.enter_context(nc.semaphore(name))

        wq_hi, wq_lo = sb("wq_hi", [P, KT, DM], fp32r), sb("wq_lo", [P, KT, DM], fp32r)
        wo_hi, wo_lo = sb("wo_hi", [P, KT, DM], fp32r), sb("wo_lo", [P, KT, DM], fp32r)
        keys_hi, keys_lo = sb("keys_hi", [P, G, CTX_ROWS], fp32r), sb("keys_lo", [P, G, CTX_ROWS], fp32r)
        values = sb("values", [P, BATCHES, HEADS // 2, DK], fp32)
        kbd_hi, kbd_lo = sb("kbd_hi", [P, G, HG * KEYS], fp32r), sb("kbd_lo", [P, G, HG * KEYS], fp32r)
        vbd_hi, vbd_lo = sb("vbd_hi", [P, G, PAIRS * P], fp32r), sb("vbd_lo", [P, G, PAIRS * P], fp32r)
        bias_row, gamma_row, beta_row = (sb(n, [P, DM], fp32) for n in ("bias_row", "gamma_row", "beta_row"))
        ident = sb("ident", [P, P], fp32)
        minus_half = sb("minus_half", [P, 1], fp32)
        xT_raw = sb("xT_raw", [P, KT, CHUNK], fp32)
        x_hi, x_lo = sb("x_hi", [P, 2, KT, CHUNK], fp32r), sb("x_lo", [P, 2, KT, CHUNK], fp32r)
        q_hi, q_lo = sb("q_hi", [P, 2, CHUNK], fp32r), sb("q_lo", [P, 2, CHUNK], fp32r)
        shifted = sb("shifted", [P, UNITS, CHUNK], fp32)
        row_max, row_sum, row_inv = (sb(n, [P, UNITS, UH], fp32) for n in ("row_max", "row_sum", "row_inv"))
        pT_hi, pT_lo = sb("pT_hi", [P, PAIRS, CHUNK], fp32r), sb("pT_lo", [P, PAIRS, CHUNK], fp32r)
        x_raw = sb("x_raw", [P, 2, DM], fp32)
        z = sb("z", [P, 2, DM], fp32)
        y = sb("y", [P, 2, DM], fp32)
        stats = sb("stats", [P, 2, 6], fp32)
        mean_var = sb("mean_var", [P, 2, 2], fp32)
        neg_mean, var_eps, rstd, shift = (sb(n, [P, 2], fp32) for n in ("neg_mean", "var_eps", "rstd", "shift"))
        with ExitStack() as first:
            ctx_raw, wk_raw, wv_raw, wqo_raw = (
                sb(n, [P, KT, DM], fp32, first) for n in ("ctx_raw", "wk_raw", "wv_raw", "wqo_raw"))
        c_hi, c_lo = sb("c_hi", [P, 2, G, CHUNK], fp32r), sb("c_lo", [P, 2, G, CHUNK], fp32r)
        probs = sb("probs", [P, G, G, HG * KEYS], fp32)

        psum = {n: ctx.enter_context(nc.psum_tensor(n, [P, 512], fp32))
                for n in ("ps_q0", "ps_q1", "ps_s0", "ps_s1", "ps_t0", "ps_t1", "ps_c", "ps_o")}
        ps_q = [psum["ps_q0"], psum["ps_q1"]]
        ps_s = [psum["ps_s0"], psum["ps_s1"]]
        ps_t = [psum["ps_t0"], psum["ps_t1"]]
        ps_c, ps_o = psum["ps_c"], psum["ps_o"]
        ps_k = [ps_q[0], ps_q[1], ps_s[0], ps_s[1]]
        ps_v = [ps_t[0], ps_t[1], ps_c, ps_o]

        ctx_loaded, wk_loaded, wv_loaded, wq_loaded, wo_loaded = (
            [sem(f"{n}_loaded{k}") for k in range(KT)] for n in ("ctx", "wk", "wv", "wq", "wo"))
        rows_loaded = sem("rows_loaded")
        xT_loaded = [sem(f"xT_loaded{k}") for k in range(KT)]
        x_loaded = [sem(f"x_loaded{s}") for s in range(2)]
        y_stored = [sem(f"y_stored{s}") for s in range(2)]
        blocks_zeroed, ident_zeroed, ident_done = sem("blocks_zeroed"), sem("ident_zeroed"), sem("ident_done")
        keys_product, keys_hi_done, keys_lo_done = sem("keys_product"), sem("keys_hi_done"), sem("keys_lo_done")
        values_product, values_done = sem("values_product"), sem("values_done")
        wq_hi_done, wq_lo_done, wo_hi_done, wo_lo_done = (
            sem(n) for n in ("wq_hi_done", "wq_lo_done", "wo_hi_done", "wo_lo_done"))
        x_hi_done, x_lo_done = sem("x_hi_done"), sem("x_lo_done")
        q_product, q_hi_done, q_lo_done = sem("q_product"), sem("q_hi_done"), sem("q_lo_done")
        kbd_done, vbd_hi_done, vbd_lo_done = sem("kbd_done"), sem("vbd_hi_done"), sem("vbd_lo_done")
        scores_done, max_done, shifted_done, exp_done = (
            sem(n) for n in ("scores_done", "max_done", "shifted_done", "exp_done"))
        sum_done, inv_done, probs_done = sem("sum_done"), sem("inv_done"), sem("probs_done")
        pT_done, pT_hi_done, pT_lo_done = sem("pT_done"), sem("pT_hi_done"), sem("pT_lo_done")
        c_product, c_hi_done, c_lo_done = sem("c_product"), sem("c_hi_done"), sem("c_lo_done")
        o_product, biased_done, z_done = sem("o_product"), sem("biased_done"), sem("z_done")
        stats_done, mean_var_done, moments_done = sem("stats_done"), sem("mean_var_done"), sem("moments_done")
        rstd_done, shift_done, normed_done, scaled_done, y_done = (
            sem(n) for n in ("rstd_done", "shift_done", "normed_done", "scaled_done", "y_done"))

        def value_blocks(t, half, g):
            return t[64 * half:64 * half + 64, g, :].rearrange("p (x c) -> p x c", c=64)[
                :, 0:4:3, DK * half:DK * half + DK]

        block = ctx.enter_context(nc.Block())

        @block.sync
        def _(sp):
            for k in range(KT):
                sp.dma_start(ctx_raw[:, k, :], ctxT_v[k, :, :]).then_inc(ctx_loaded[k], 16)
                sp.dma_start(wk_raw[:, k, :], wkT_v[k, :, :]).then_inc(wk_loaded[k], 16)
            for k in range(KT):
                sp.dma_start(xT_raw[:, k, :], xT_v[k, :, 0:CHUNK]).then_inc(xT_loaded[k], 16)
                sp.dma_start(wqo_raw[:, k, :], wqT_v[k, :, :]).then_inc(wq_loaded[k], 16)
            for k in range(KT):
                sp.dma_start(wv_raw[:, k, :], wvT_v[k, :, :]).then_inc(wv_loaded[k], 16)
            for row, src in ((bias_row, b_o), (gamma_row, gamma), (beta_row, beta)):
                sp.dma_start(row[:, :], src.partition_broadcast(P)).then_inc(rows_loaded, 16)
            for s in range(2):
                sp.dma_start(x_raw[:, s, :], x[s * P:(s + 1) * P, :]).then_inc(x_loaded[s], 16)

            for k in range(KT):
                sp.wait_ge(wq_lo_done, k + 1)
                sp.dma_start(wqo_raw[:, k, :], woT_v[k, :, :]).then_inc(wo_loaded[k], 16)

            def slot(st, g):
                c = st.c
                tile = 4 * (c - 1) + g
                if not isinstance(c, int) or c + 3 < CHUNKS:
                    wait(sp, x_lo_done, 4 * (c + 2) + g + 1)
                    sp.dma_start(xT_raw[:, g, :], xT_v[g, :, bass.ds(CHUNK * (c + 3), CHUNK)]
                                 ).then_inc(xT_loaded[g], 16)
                if st.output:
                    if not isinstance(c, int) or tile + 2 < TILES:
                        wait(sp, biased_done, tile + 1)
                        sp.dma_start(x_raw[:, g % 2, :], x[bass.ds(P * (tile + 2), P), :]
                                     ).then_inc(x_loaded[g % 2], 16)
                    if not isinstance(c, int) or tile > 0:
                        wait(sp, y_done, tile)
                        sp.dma_start(out[bass.ds(P * (tile - 1), P), :], y[:, 1 - g % 2, :]
                                     ).then_inc(y_stored[1 - g % 2], 16)

            all_steps(sp, slot)
            sp.wait_ge(y_done, TILES)
            sp.dma_start(out[P * (TILES - 1):P * TILES, :], y[:, 1, :]).then_inc(y_stored[1], 16)
            for s in range(2):
                sp.wait_ge(y_stored[s], 16 * TILES // 2)

        @block.tensor
        def _(pe):
            for g in range(G):
                for k in range(KT):
                    if g == 0:
                        pe.wait_ge(wk_loaded[k], 16)
                        pe.wait_ge(ctx_loaded[k], 16)
                    mm = nc.tensor.matmul(ps_k[g][:, :], wk_raw[:, k, g * P:(g + 1) * P], ctx_raw[:, k, :],
                                          start=(k == 0), stop=(k == KT - 1))
                mm.then_inc(keys_product, 1)

            def project_values():
                for b2 in range(BATCHES // 2):
                    for k in range(KT):
                        if b2 == 0:
                            pe.wait_ge(wv_loaded[k], 16)
                        mm = nc.tensor.matmul(ps_v[b2][:, :], ctx_raw[:, k, b2 * P:(b2 + 1) * P], wv_raw[:, k, :],
                                              start=(k == 0), stop=(k == KT - 1))
                    mm.then_inc(values_product, 1)

            def three_passes(dst, pairs):
                last = len(pairs) * 3 - 1
                n = 0
                for (l_hi, l_lo), (r_hi, r_lo) in pairs:
                    for lhs, rhs in ((l_lo, r_hi), (l_hi, r_lo), (l_hi, r_hi)):
                        mm = nc.tensor.matmul(dst, lhs, rhs, start=(n == 0), stop=(n == last))
                        n += 1
                return mm

            def slot(st, g):
                c = st.c
                if st.stage1:
                    n = 4 * (c + 1) + g
                    par = 1 - st.odd
                    if g == 0:
                        wait(pe, x_lo_done, n + 4)
                        if isinstance(c, int) and c == -1:
                            pe.wait_ge(wq_lo_done, KT)
                    if isinstance(c, int) and c == -1:
                        pe.wait_ge(keys_lo_done, g + 1 if g < 2 else 1)
                    wait(pe, q_lo_done, n - 1)
                    three_passes(ps_q[g % 2][:, :], [
                        ((wq_hi[:, k, g * P:(g + 1) * P], wq_lo[:, k, g * P:(g + 1) * P]),
                         (x_hi[:, par, k, :], x_lo[:, par, k, :])) for k in range(KT)]).then_inc(q_product, 1)
                if st.stage2:
                    n = 8 * c + 2 * g
                    wait(pe, probs_done, n + 2)
                    if isinstance(c, int) and c == 0 and g == 0:
                        pe.wait_ge(ident_done, 1)
                        pe.wait_ge(values_done, 4)
                    for pair in range(PAIRS):
                        wait(pe, pT_lo_done, n + pair - 1)
                        for t in range(G):
                            mm = nc.tensor.transpose(ps_t[pair][:, t * P:(t + 1) * P],
                                                     probs[:, g, t, pair * P:(pair + 1) * P], ident[:, :])
                        mm.then_inc(pT_done, 1)
                if st.output:
                    n = 4 * (c - 1) + g
                    par = 1 - st.odd
                    if g == 0:
                        wait(pe, c_lo_done, n + 4)
                        if isinstance(c, int) and c == 1:
                            pe.wait_ge(wo_lo_done, KT)
                    wait(pe, z_done, n)
                    three_passes(ps_o[:, :], [
                        ((c_hi[:, par, k, g * P:(g + 1) * P], c_lo[:, par, k, g * P:(g + 1) * P]),
                         (wo_hi[:, k, :], wo_lo[:, k, :])) for k in range(KT)]).then_inc(o_product, 1)
                if st.stage1:
                    n = 4 * (c + 1) + g
                    wait(pe, q_lo_done, n + 1)
                    if st.odd:
                        wait(pe, kbd_done, 4 * st.batch + g + 1)
                    if isinstance(c, int) and c == -1 and g == 0:
                        pe.wait_ge(keys_lo_done, G)
                    for u in range(UNITS):
                        wait(pe, shifted_done, 2 * n + u - 1)
                        for t in range(2):
                            rows = slice((2 * u + t) * P, (2 * u + t + 1) * P)
                            mm = three_passes(ps_s[u][:, t * 256:(t + 1) * 256], [
                                ((q_hi[:, g % 2, rows], q_lo[:, g % 2, rows]),
                                 (kbd_hi[:, g, :], kbd_lo[:, g, :]))])
                        mm.then_inc(scores_done, 1)
                if st.stage2:
                    n = 4 * c + g
                    wait(pe, pT_lo_done, 2 * n + 2)
                    wait(pe, c_lo_done, n)
                    if not st.odd:
                        wait(pe, vbd_lo_done, 4 * st.batch + g + 1)
                    three_passes(ps_c[:, :], [
                        ((vbd_hi[:, g, pair * P:(pair + 1) * P], vbd_lo[:, g, pair * P:(pair + 1) * P]),
                         (pT_hi[:, pair, :], pT_lo[:, pair, :])) for pair in range(PAIRS)]).then_inc(c_product, 1)
                if isinstance(c, int) and c == -1 and g == G - 1:
                    project_values()

            all_steps(pe, slot)

        @block.scalar
        def _(act):
            def to_hi(dst, src):
                return nc.scalar.activation(dst, src, ACT.Copy)

            for g in range(G):
                act.wait_ge(keys_product, g + 1)
                to_hi(keys_hi[:, g, :], ps_k[g][:, :]).then_inc(keys_hi_done, 1)
            for k in range(KT):
                act.wait_ge(wq_loaded[k], 16)
                to_hi(wq_hi[:, k, :], wqo_raw[:, k, :]).then_inc(wq_hi_done, 1)

            def enter_values(batch, c, g):
                wait(act, c_product, 4 * c + g + 1)
                for half in range(2):
                    src = values[64 * half:64 * half + 64, bass.ds(batch, 1), PAIRS * g:PAIRS * (g + 1), :]
                    last = to_hi(value_blocks(vbd_hi, half, g), src.rearrange("p b r d -> p (b r) d"))
                last.then_inc(vbd_hi_done, 1)

            def slot(st, g):
                c = st.c
                first = isinstance(c, int) and c == -1
                if st.split:
                    n = 4 * (c + 2) + g
                    wait(act, xT_loaded[g], 16 * (c + 3))
                    if g == 0:
                        wait(act, q_product, 4 * c + 4)
                    to_hi(x_hi[:, st.odd, g, :], xT_raw[:, g, :]).then_inc(x_hi_done, 1)
                if st.stage1:
                    n = 4 * (c + 1) + g
                    wait(act, scores_done, 2 * (n - 1))
                    wait(act, q_product, n + 1)
                    to_hi(q_hi[:, g % 2, :], ps_q[g % 2][:, :]).then_inc(q_hi_done, 1)
                if st.stage2:
                    wait(act, c_product, 4 * c + g)
                    for pair in range(PAIRS):
                        wait(act, pT_done, 8 * c + 2 * g + pair + 1)
                        to_hi(pT_hi[:, pair, :], ps_t[pair][:, :]).then_inc(pT_hi_done, 1)
                if st.stage1:
                    n = 8 * (c + 1) + 2 * g
                    wait(act, pT_done, n - 6)
                    for u in range(UNITS):
                        wait(act, shifted_done, n + u + 1)
                        nc.scalar.activation(
                            probs[:, g, 2 * u:2 * u + 2, :],
                            shifted[:, u, :].rearrange("p (t n) -> p t n", t=2),
                            ACT.Exp, scale=SCALE).then_inc(exp_done, 1)
                if st.output:
                    n = 4 * (c - 1) + g
                    s = g % 2
                    wait(act, shift_done, n + 1)
                    wait(act, y_stored[s], 16 * (2 * (c - 1) + g // 2))
                    nc.scalar.activation(y[:, s, :], z[:, s, :], ACT.Identity, bias=shift[:, s:s + 1],
                                         scale=rstd[:, s:s + 1]).then_inc(normed_done, 1)
                if st.stage2:
                    n = 4 * c + g
                    if g == 0:
                        wait(act, o_product, 4 * (c - 1))
                    wait(act, c_product, n + 1)
                    to_hi(c_hi[:, st.odd, g, :], ps_c[:, :]).then_inc(c_hi_done, 1)
                if st.next_keys:
                    wait(act, scores_done, 8 * (c + 1) + 2 * g + 2)
                    if isinstance(c, int) and c == -2 and g == 0:
                        act.wait_ge(keys_lo_done, G)
                        act.wait_ge(blocks_zeroed, 4)
                    for whole, bd in ((keys_hi, kbd_hi), (keys_lo, kbd_lo)):
                        for j in range(HG):
                            rows = slice(DK * j, DK * j + DK)
                            last = to_hi(bd[rows, g, KEYS * j:KEYS * (j + 1)],
                                         whole[rows, g, bass.ds(KEYS * (st.batch + 1), KEYS)].bitcast(fp32))
                    last.then_inc(kbd_done, 1)
                if st.next_values and not first:
                    enter_values(st.batch, c, g)
                if first and g == G - 1:
                    for b2 in range(BATCHES // 2):
                        act.wait_ge(values_product, b2 + 1)
                        for b in range(2):
                            for half in range(2):
                                src = ps_v[b2][KEYS * b:KEYS * (b + 1), :].rearrange(
                                    "p (r h d) -> p r h d", h=2, d=DK)[:, :, half, :]
                                last = nc.scalar.activation(
                                    values[64 * half:64 * half + 64, 2 * b2 + b, :, :], src, ACT.Copy)
                        last.then_inc(values_done, 1)
                    act.wait_ge(values_done, 4)
                    for group in range(G):
                        enter_values(0, c, group)
                    for k in range(KT):
                        act.wait_ge(wo_loaded[k], 16)
                        to_hi(wo_hi[:, k, :], wqo_raw[:, k, :]).then_inc(wo_hi_done, 1)

            all_steps(act, slot)

        @block.vector
        def _(dve):
            def to_lo(dst, whole, hi):
                return nc.vector.tensor_tensor(dst, whole, hi.bitcast(fp32), ALU.subtract)

            for t in (kbd_hi, kbd_lo, vbd_hi, vbd_lo):
                nc.vector.memset(t[:, :, :].bitcast(fp32), 0.0).then_inc(blocks_zeroed, 1)
            for k in range(KT):
                dve.wait_ge(wq_hi_done, k + 1)
                to_lo(wq_lo[:, k, :], wqo_raw[:, k, :], wq_hi[:, k, :]).then_inc(wq_lo_done, 1)
                if k == 0:
                    for g in range(G):
                        dve.wait_ge(keys_hi_done, g + 1)
                        to_lo(keys_lo[:, g, :], ps_k[g][:, :], keys_hi[:, g, :]).then_inc(keys_lo_done, 1)

            def enter_values(batch, g):
                dve.wait_ge(vbd_hi_done, 4 * batch + g + 1)
                for half in range(2):
                    src = values[64 * half:64 * half + 64, bass.ds(batch, 1), PAIRS * g:PAIRS * (g + 1), :]
                    last = to_lo(value_blocks(vbd_lo, half, g), src.rearrange("p b r d -> p (b r) d"),
                                 value_blocks(vbd_hi, half, g))
                last.then_inc(vbd_lo_done, 1)

            def slot(st, g):
                c = st.c
                first = isinstance(c, int) and c == -1
                if st.stage1:
                    n = 4 * (c + 1) + g
                    dve.wait_ge(q_hi_done, n + 1)
                    to_lo(q_lo[:, g % 2, :], ps_q[g % 2][:, :], q_hi[:, g % 2, :]).then_inc(q_lo_done, 1)
                if st.stage2:
                    for pair in range(PAIRS):
                        dve.wait_ge(pT_hi_done, 8 * c + 2 * g + pair + 1)
                        to_lo(pT_lo[:, pair, :], ps_t[pair][:, :], pT_hi[:, pair, :]).then_inc(pT_lo_done, 1)
                if st.output:
                    n = 4 * (c - 1) + g
                    s = g % 2
                    dve.wait_ge(o_product, n + 1)
                    dve.wait_ge(biased_done, n + 1)
                    nc.vector.tensor_tensor(z[:, s, :], ps_o[:, :], z[:, s, :], ALU.add).then_inc(z_done, 1)
                    dve.wait_ge(z_done, n + 1)
                    nc.vector.bn_stats(stats[:, s, :], z[:, s, :]).then_inc(stats_done, 1)
                if st.stage1:
                    n = 8 * (c + 1) + 2 * g
                    for u in range(UNITS):
                        if st.output and u == 1:
                            dve.wait_ge(stats_done, 4 * (c - 1) + g + 1)
                        dve.wait_ge(scores_done, n + u + 1)
                        nc.vector.tensor_reduce(row_max[:, u, :], ps_s[u][:, :].rearrange("p (h k) -> p h k", k=KEYS),
                                                axis=AX.X, op=ALU.max).then_inc(max_done, 1)
                if st.output:
                    n = 4 * (c - 1) + g
                    s = g % 2
                    if not st.stage1:
                        dve.wait_ge(stats_done, n + 1)
                    nc.vector.bn_aggr(mean_var[:, s, :], stats[:, s, :]).then_inc(mean_var_done, 1)
                if st.stage1:
                    n = 8 * (c + 1) + 2 * g
                    for u in range(UNITS):
                        dve.wait_ge(max_done, n + u + 1)
                        wait(dve, exp_done, n + u - 1)
                        nc.vector.tensor_tensor(
                            shifted[:, u, :].rearrange("p (h k) -> p h k", k=KEYS),
                            ps_s[u][:, :].rearrange("p (h k) -> p h k", k=KEYS),
                            row_max[:, u, :].unsqueeze(2).to_broadcast([P, UH, KEYS]),
                            ALU.subtract).then_inc(shifted_done, 1)
                if st.output:
                    n = 4 * (c - 1) + g
                    s = g % 2
                    dve.wait_ge(mean_var_done, n + 1)
                    nc.vector.tensor_scalar(var_eps[:, s:s + 1], mean_var[:, s, 1:2], EPS, None, ALU.add)
                    nc.vector.tensor_scalar(neg_mean[:, s:s + 1], mean_var[:, s, 0:1], -1.0, None,
                                            ALU.mult).then_inc(moments_done, 1)
                if st.stage1:
                    n = 8 * (c + 1) + 2 * g
                    for u in range(UNITS):
                        dve.wait_ge(exp_done, n + u + 1)
                        nc.vector.tensor_reduce(
                            row_sum[:, u, :].rearrange("p (t h) -> p t h", t=2),
                            probs[:, g, 2 * u:2 * u + 2, :].rearrange("p t (h k) -> p t h k", k=KEYS),
                            axis=AX.X, op=ALU.add).then_inc(sum_done, 1)
                if st.stage2:
                    n = 4 * c + g
                    dve.wait_ge(c_hi_done, n + 1)
                    to_lo(c_lo[:, st.odd, g, :], ps_c[:, :], c_hi[:, st.odd, g, :]).then_inc(c_lo_done, 1)
                if st.stage1:
                    n = 8 * (c + 1) + 2 * g
                    dve.wait_ge(sum_done, n + 2)
                    wait(dve, probs_done, n)
                    nc.vector.reciprocal(row_inv[:, :, :], row_sum[:, :, :]).then_inc(inv_done, 1)
                if st.next_values and not first:
                    enter_values(st.batch, g)
                if first and g == G - 1:
                    for group in range(G):
                        enter_values(0, group)
                    for k in range(KT):
                        dve.wait_ge(wo_hi_done, k + 1)
                        to_lo(wo_lo[:, k, :], wqo_raw[:, k, :], wo_hi[:, k, :]).then_inc(wo_lo_done, 1)

            all_steps(dve, slot)

        @block.gpsimd
        def _(pool):
            nc.gpsimd.memset(minus_half[:, :], -0.5)
            nc.gpsimd.memset(ident[:, :], 0.0).then_inc(ident_zeroed, 1)
            pool.wait_ge(ident_zeroed, 1)
            nc.gpsimd.affine_select(out=ident[:, :], in_=ident[:, :], compare_op=ALU.not_equal, fill=1.0,
                                    base=0, pattern=[[-1, P]], channel_multiplier=1).then_inc(ident_done, 1)
            pool.wait_ge(ident_done, 1)

            def slot(st, g):
                c = st.c
                if st.output:
                    n = 4 * (c - 1) + g
                    s = g % 2
                    if isinstance(c, int) and c == 1 and g == 0:
                        pool.wait_ge(rows_loaded, 48)
                    wait(pool, x_loaded[s], 16 * (2 * (c - 1) + g // 2 + 1))
                    wait(pool, normed_done, n - 1)
                    nc.gpsimd.tensor_tensor(z[:, s, :], x_raw[:, s, :], bias_row[:, :], ALU.add
                                            ).then_inc(biased_done, 1)
                if st.split:
                    n = 4 * (c + 2) + g
                    pool.wait_ge(x_hi_done, n + 1)
                    nc.gpsimd.tensor_tensor(x_lo[:, st.odd, g, :], xT_raw[:, g, :],
                                            x_hi[:, st.odd, g, :].bitcast(fp32), ALU.subtract
                                            ).then_inc(x_lo_done, 1)
                if st.output:
                    n = 4 * (c - 1) + g
                    s = g % 2
                    pool.wait_ge(moments_done, n + 1)
                    nc.gpsimd.tensor_tensor(rstd[:, s:s + 1], var_eps[:, s:s + 1], minus_half[:, :], ALU.pow
                                            ).then_inc(rstd_done, 1)
                    pool.wait_ge(rstd_done, n + 1)
                    nc.gpsimd.tensor_tensor(shift[:, s:s + 1], neg_mean[:, s:s + 1], rstd[:, s:s + 1], ALU.mult
                                            ).then_inc(shift_done, 1)
                if st.stage1:
                    pool.wait_ge(inv_done, 4 * (c + 1) + g + 1)
                    for u in range(UNITS):
                        part = probs[:, g, 2 * u:2 * u + 2, :].rearrange("p t (h k) -> p t h k", k=KEYS)
                        inv = row_inv[:, u, :].rearrange("p (t h) -> p t h", t=2)
                        nc.gpsimd.tensor_tensor(part, part, inv.unsqueeze(3).to_broadcast([P, 2, HG, KEYS]),
                                                ALU.mult).then_inc(probs_done, 1)
                if st.output:
                    n = 4 * (c - 1) + g
                    s = g % 2
                    pool.wait_ge(normed_done, n + 1)
                    nc.gpsimd.tensor_tensor(y[:, s, :], y[:, s, :], gamma_row[:, :], ALU.mult
                                            ).then_inc(scaled_done, 1)
                    pool.wait_ge(scaled_done, n + 1)
                    nc.gpsimd.tensor_tensor(y[:, s, :], y[:, s, :], beta_row[:, :], ALU.add
                                            ).then_inc(y_done, 1)

            all_steps(pool, slot)


def kernel(x, ctx_1024, L0_xattn_w_q, L0_xattn_w_k, L0_xattn_w_v, L0_xattn_w_o, L0_xattn_b_o,
           L0_xattn_ln_gamma, L0_xattn_ln_beta):
    import numpy as np
    import concourse.bacc as bacc
    from concourse.bass_utils import run_bass_kernel_spmd

    x = np.asarray(x)
    rows = x.reshape(-1, x.shape[-1])
    ctx_rows = np.asarray(ctx_1024).reshape(-1, x.shape[-1])
    arrays = {"xT": rows.T, "x": rows, "ctxT": ctx_rows.T,
              "wqT": np.asarray(L0_xattn_w_q).T, "wkT": np.asarray(L0_xattn_w_k).T,
              "wvT": np.asarray(L0_xattn_w_v).T, "woT": np.asarray(L0_xattn_w_o).T,
              "b_o": np.asarray(L0_xattn_b_o), "gamma": np.asarray(L0_xattn_ln_gamma),
              "beta": np.asarray(L0_xattn_ln_beta)}
    arrays = {f"in_{name}": np.ascontiguousarray(a) for name, a in arrays.items()}
    nc = bacc.Bacc("TRN2", target_bir_lowering=False, num_devices=1)
    args = [nc.dram_tensor(name, a.shape, mybir.dt.from_np(a.dtype), kind="ExternalInput").ap()
            for name, a in arrays.items()]
    out = nc.dram_tensor("out", rows.shape, mybir.dt.from_np(rows.dtype), kind="ExternalOutput").ap()
    cross_attention_kernel(nc, *args, out)
    result = run_bass_kernel_spmd(nc, [arrays], core_ids=[0])
    return result.results[0]["out"].reshape(x.shape)
```

```python
from collections import namedtuple
from contextlib import ExitStack

import concourse.bass as bass
from concourse import mybir

Step = namedtuple("Step", "c odd batch split stage1 stage2 output next_keys next_values")


def cross_attention_kernel(nc, xT, x, ctxT, wqT, wkT, wvT, woT, b_o, gamma, beta, out):
    fp32, fp32r = mybir.dt.float32, mybir.dt.float32r
    ALU, ACT, AX = mybir.AluOpType, mybir.ActivationFunctionType, mybir.AxisListType

    P = 128
    DM, ROWS = xT.shape
    CTX_ROWS = ctxT.shape[1]
    BATCHES, HEADS = 8, 16
    KEYS = CTX_ROWS // BATCHES
    DK = DM // HEADS
    KT = DM // P
    CHUNK = 512
    CHUNKS = ROWS // CHUNK
    G = KT
    HG = HEADS // G
    PAIRS = HG // 2
    UNITS = 2
    UH = UNITS * HG
    TILES = CHUNKS * G
    SCALE = float(DK) ** -0.5
    EPS = 1e-5
    assert CHUNKS == 2 * BATCHES and G == CHUNK // P and 2 * KEYS == P and KT * P == DM

    def step_of(c, odd, batch, whole=False):
        if whole:
            return Step(c, odd, batch, True, True, True, True, not odd, odd)
        return Step(c, odd, batch, 0 <= c + 2 < CHUNKS, 0 <= c + 1 < CHUNKS, 0 <= c < CHUNKS,
                    0 <= c - 1 < CHUNKS, not odd and 0 <= batch + 1 < BATCHES, odd and 0 <= batch < BATCHES)

    def all_slots(slot):
        def quarters(eng_step, before):
            for g in range(G):
                slot(eng_step, g, before if g == 0 else eng_step, (g - 1) % G)
        return quarters

    def all_steps(eng, slot):
        quarters = all_slots(slot)

        def fixed(c):
            return step_of(c, c % 2, (c + 1) // 2)

        for c in range(-2, 3):
            quarters(fixed(c), fixed(c - 1))
        with eng.Fori(1, BATCHES - 2) as i:
            even, odd = step_of(2 * i, 0, i, whole=True), step_of(2 * i + 1, 1, i + 1, whole=True)
            quarters(odd, even)
            quarters(step_of(2 * i + 2, 0, i + 1, whole=True), odd)
        for c in range(CHUNKS - 3, CHUNKS + 1):
            quarters(fixed(c), fixed(c - 1))
        slot(fixed(CHUNKS + 1), 0, fixed(CHUNKS), G - 1)

    def wait(eng, sem, value):
        if not isinstance(value, int) or value > 0:
            eng.wait_ge(sem, value)

    xT_v = xT.rearrange("(k p) n -> k p n", p=P)
    ctxT_v, wqT_v, wkT_v, wvT_v, woT_v = (
        a.rearrange("(k p) n -> k p n", p=P) for a in (ctxT, wqT, wkT, wvT, woT))

    with ExitStack() as ctx:
        def sb(name, shape, dt, stack=ctx):
            return stack.enter_context(nc.sbuf_tensor(name, shape, dt))

        def sem(name):
            return ctx.enter_context(nc.semaphore(name))

        wq_hi, wq_lo = sb("wq_hi", [P, KT, DM], fp32r), sb("wq_lo", [P, KT, DM], fp32r)
        wo_hi, wo_lo = sb("wo_hi", [P, KT, DM], fp32r), sb("wo_lo", [P, KT, DM], fp32r)
        keys_hi, keys_lo = sb("keys_hi", [P, G, CTX_ROWS], fp32r), sb("keys_lo", [P, G, CTX_ROWS], fp32r)
        values = sb("values", [P, BATCHES, HEADS // 2, DK], fp32)
        kbd_hi, kbd_lo = sb("kbd_hi", [P, G, HG * KEYS], fp32r), sb("kbd_lo", [P, G, HG * KEYS], fp32r)
        vbd_hi, vbd_lo = sb("vbd_hi", [P, G, PAIRS * P], fp32r), sb("vbd_lo", [P, G, PAIRS * P], fp32r)
        bias_row, gamma_row, beta_row = (sb(n, [P, DM], fp32) for n in ("bias_row", "gamma_row", "beta_row"))
        ident = sb("ident", [P, P], fp32)
        minus_half = sb("minus_half", [P, 1], fp32)
        xT_raw = sb("xT_raw", [P, KT, CHUNK], fp32)
        x_hi, x_lo = sb("x_hi", [P, 2, KT, CHUNK], fp32r), sb("x_lo", [P, 2, KT, CHUNK], fp32r)
        q_hi, q_lo = sb("q_hi", [P, 2, CHUNK], fp32r), sb("q_lo", [P, 2, CHUNK], fp32r)
        shifted = sb("shifted", [P, UNITS, CHUNK], fp32)
        row_max, row_sum, row_inv = (sb(n, [P, UNITS, UH], fp32) for n in ("row_max", "row_sum", "row_inv"))
        pT_hi, pT_lo = sb("pT_hi", [P, PAIRS, CHUNK], fp32r), sb("pT_lo", [P, PAIRS, CHUNK], fp32r)
        x_raw = sb("x_raw", [P, 2, DM], fp32)
        z = sb("z", [P, 2, DM], fp32)
        y = sb("y", [P, 2, DM], fp32)
        stats = sb("stats", [P, 2, 6], fp32)
        mean_var = sb("mean_var", [P, 2, 2], fp32)
        neg_mean, var_eps, rstd, shift = (sb(n, [P, 2], fp32) for n in ("neg_mean", "var_eps", "rstd", "shift"))
        with ExitStack() as first:
            ctx_raw, wk_raw, wv_raw, wqo_raw = (
                sb(n, [P, KT, DM], fp32, first) for n in ("ctx_raw", "wk_raw", "wv_raw", "wqo_raw"))
        c_hi, c_lo = sb("c_hi", [P, 2, G, CHUNK], fp32r), sb("c_lo", [P, 2, G, CHUNK], fp32r)
        probs = sb("probs", [P, G, G, HG * KEYS], fp32)

        psum = {n: ctx.enter_context(nc.psum_tensor(n, [P, 512], fp32))
                for n in ("ps_q0", "ps_q1", "ps_s0", "ps_s1", "ps_t0", "ps_t1", "ps_c", "ps_o")}
        ps_q = [psum["ps_q0"], psum["ps_q1"]]
        ps_s = [psum["ps_s0"], psum["ps_s1"]]
        ps_t = [psum["ps_t0"], psum["ps_t1"]]
        ps_c, ps_o = psum["ps_c"], psum["ps_o"]
        ps_k = [ps_q[0], ps_q[1], ps_s[0], ps_s[1]]
        ps_v = [ps_t[0], ps_t[1], ps_c, ps_o]

        ctx_loaded, wk_loaded, wv_loaded, wq_loaded, wo_loaded = (
            [sem(f"{n}_loaded{k}") for k in range(KT)] for n in ("ctx", "wk", "wv", "wq", "wo"))
        rows_loaded = sem("rows_loaded")
        xT_loaded = [sem(f"xT_loaded{k}") for k in range(KT)]
        x_loaded = [sem(f"x_loaded{s}") for s in range(2)]
        y_stored = [sem(f"y_stored{s}") for s in range(2)]
        blocks_zeroed, ident_zeroed, ident_done = sem("blocks_zeroed"), sem("ident_zeroed"), sem("ident_done")
        keys_product, keys_hi_done, keys_lo_done = sem("keys_product"), sem("keys_hi_done"), sem("keys_lo_done")
        values_product, values_done = sem("values_product"), sem("values_done")
        wq_hi_done, wq_lo_done, wo_hi_done, wo_lo_done = (
            sem(n) for n in ("wq_hi_done", "wq_lo_done", "wo_hi_done", "wo_lo_done"))
        x_hi_done, x_lo_done = sem("x_hi_done"), sem("x_lo_done")
        q_product, q_hi_done, q_lo_done = sem("q_product"), sem("q_hi_done"), sem("q_lo_done")
        kbd_done, vbd_hi_done, vbd_lo_done = sem("kbd_done"), sem("vbd_hi_done"), sem("vbd_lo_done")
        scores_done, max_done, shifted_done, exp_done = (
            sem(n) for n in ("scores_done", "max_done", "shifted_done", "exp_done"))
        sum_done, inv_done, probs_done = sem("sum_done"), sem("inv_done"), sem("probs_done")
        pT_done, pT_hi_done, pT_lo_done = sem("pT_done"), sem("pT_hi_done"), sem("pT_lo_done")
        c_product, c_hi_done, c_lo_done = sem("c_product"), sem("c_hi_done"), sem("c_lo_done")
        o_product, biased_done, z_done = sem("o_product"), sem("biased_done"), sem("z_done")
        stats_done, mean_var_done, moments_done = sem("stats_done"), sem("mean_var_done"), sem("moments_done")
        rstd_done, shift_done, normed_done, scaled_done, y_done = (
            sem(n) for n in ("rstd_done", "shift_done", "normed_done", "scaled_done", "y_done"))

        def value_blocks(t, half, g):
            return t[64 * half:64 * half + 64, g, :].rearrange("p (x c) -> p x c", c=64)[
                :, 0:4:3, DK * half:DK * half + DK]

        block = ctx.enter_context(nc.Block())

        @block.sync
        def _(sp):
            for k in range(KT):
                sp.dma_start(ctx_raw[:, k, :], ctxT_v[k, :, :]).then_inc(ctx_loaded[k], 16)
                sp.dma_start(wk_raw[:, k, :], wkT_v[k, :, :]).then_inc(wk_loaded[k], 16)
            for k in range(KT):
                sp.dma_start(xT_raw[:, k, :], xT_v[k, :, 0:CHUNK]).then_inc(xT_loaded[k], 16)
                sp.dma_start(wqo_raw[:, k, :], wqT_v[k, :, :]).then_inc(wq_loaded[k], 16)
            for k in range(KT):
                sp.dma_start(wv_raw[:, k, :], wvT_v[k, :, :]).then_inc(wv_loaded[k], 16)
            for row, src in ((bias_row, b_o), (gamma_row, gamma), (beta_row, beta)):
                sp.dma_start(row[:, :], src.partition_broadcast(P)).then_inc(rows_loaded, 16)
            for s in range(2):
                sp.dma_start(x_raw[:, s, :], x[s * P:(s + 1) * P, :]).then_inc(x_loaded[s], 16)

            for k in range(KT):
                sp.wait_ge(wq_lo_done, k + 1)
                sp.dma_start(wqo_raw[:, k, :], woT_v[k, :, :]).then_inc(wo_loaded[k], 16)

            def slot(st, g, before, gb):
                c = st.c
                tile = 4 * (c - 1) + g
                if (st.output or before.output) and (not isinstance(c, int) or tile > 1):
                    wait(sp, y_done, tile - 1)
                    sp.dma_start(out[bass.ds(P * (tile - 2), P), :], y[:, g % 2, :]).then_inc(y_stored[g % 2], 16)
                if st.output and (not isinstance(c, int) or tile + 2 < TILES):
                    wait(sp, biased_done, tile + 1)
                    sp.dma_start(x_raw[:, g % 2, :], x[bass.ds(P * (tile + 2), P), :]
                                 ).then_inc(x_loaded[g % 2], 16)
                if st.split and (not isinstance(c, int) or c + 3 < CHUNKS):
                    wait(sp, x_lo_done, 4 * (c + 2) + g + 1)
                    sp.dma_start(xT_raw[:, g, :], xT_v[g, :, bass.ds(CHUNK * (c + 3), CHUNK)]
                                 ).then_inc(xT_loaded[g], 16)

            all_steps(sp, slot)
            sp.wait_ge(y_done, TILES)
            sp.dma_start(out[P * (TILES - 1):P * TILES, :], y[:, 1, :]).then_inc(y_stored[1], 16)
            for s in range(2):
                sp.wait_ge(y_stored[s], 16 * TILES // 2)

        @block.tensor
        def _(pe):
            for g in range(G):
                for k in range(KT):
                    if g == 0:
                        pe.wait_ge(wk_loaded[k], 16)
                        pe.wait_ge(ctx_loaded[k], 16)
                    mm = nc.tensor.matmul(ps_k[g][:, :], wk_raw[:, k, g * P:(g + 1) * P], ctx_raw[:, k, :],
                                          start=(k == 0), stop=(k == KT - 1))
                mm.then_inc(keys_product, 1)

            def project_values():
                for b2 in range(BATCHES // 2):
                    for k in range(KT):
                        if b2 == 0:
                            pe.wait_ge(wv_loaded[k], 16)
                        mm = nc.tensor.matmul(ps_v[b2][:, :], ctx_raw[:, k, b2 * P:(b2 + 1) * P], wv_raw[:, k, :],
                                              start=(k == 0), stop=(k == KT - 1))
                    mm.then_inc(values_product, 1)

            def three_passes(dst, pairs):
                last = len(pairs) * 3 - 1
                n = 0
                for (l_hi, l_lo), (r_hi, r_lo) in pairs:
                    for lhs, rhs in ((l_lo, r_hi), (l_hi, r_lo), (l_hi, r_hi)):
                        mm = nc.tensor.matmul(dst, lhs, rhs, start=(n == 0), stop=(n == last))
                        n += 1
                return mm

            def slot(st, g, before, gb):
                c = st.c
                if st.stage1:
                    n = 4 * (c + 1) + g
                    par = 1 - st.odd
                    if g == 0:
                        wait(pe, x_lo_done, n + 4)
                        if isinstance(c, int) and c == -1:
                            pe.wait_ge(wq_lo_done, KT)
                    if isinstance(c, int) and c == -1:
                        pe.wait_ge(keys_lo_done, g + 1 if g < 2 else 1)
                    wait(pe, q_lo_done, n - 1)
                    three_passes(ps_q[g % 2][:, :], [
                        ((wq_hi[:, k, g * P:(g + 1) * P], wq_lo[:, k, g * P:(g + 1) * P]),
                         (x_hi[:, par, k, :], x_lo[:, par, k, :])) for k in range(KT)]).then_inc(q_product, 1)
                if st.stage2:
                    n = 8 * c + 2 * g
                    wait(pe, probs_done, n + 2)
                    if isinstance(c, int) and c == 0 and g == 0:
                        pe.wait_ge(ident_done, 1)
                        pe.wait_ge(values_done, 4)
                    for pair in range(PAIRS):
                        wait(pe, pT_lo_done, n + pair - 1)
                        for t in range(G):
                            mm = nc.tensor.transpose(ps_t[pair][:, t * P:(t + 1) * P],
                                                     probs[:, g, t, pair * P:(pair + 1) * P], ident[:, :])
                        mm.then_inc(pT_done, 1)
                if st.output:
                    n = 4 * (c - 1) + g
                    par = 1 - st.odd
                    if g == 0:
                        wait(pe, c_lo_done, n + 4)
                        if isinstance(c, int) and c == 1:
                            pe.wait_ge(wo_lo_done, KT)
                    wait(pe, z_done, n)
                    three_passes(ps_o[:, :], [
                        ((c_hi[:, par, k, g * P:(g + 1) * P], c_lo[:, par, k, g * P:(g + 1) * P]),
                         (wo_hi[:, k, :], wo_lo[:, k, :])) for k in range(KT)]).then_inc(o_product, 1)
                if st.stage1:
                    n = 4 * (c + 1) + g
                    wait(pe, q_lo_done, n + 1)
                    if st.odd:
                        wait(pe, kbd_done, 4 * st.batch + g + 1)
                    if isinstance(c, int) and c == -1 and g == 0:
                        pe.wait_ge(keys_lo_done, G)
                    for u in range(UNITS):
                        wait(pe, shifted_done, 2 * n + u - 1)
                        for t in range(2):
                            rows = slice((2 * u + t) * P, (2 * u + t + 1) * P)
                            mm = three_passes(ps_s[u][:, t * 256:(t + 1) * 256], [
                                ((q_hi[:, g % 2, rows], q_lo[:, g % 2, rows]),
                                 (kbd_hi[:, g, :], kbd_lo[:, g, :]))])
                        mm.then_inc(scores_done, 1)
                if st.stage2:
                    n = 4 * c + g
                    wait(pe, pT_lo_done, 2 * n + 2)
                    wait(pe, c_lo_done, n)
                    if not st.odd:
                        wait(pe, vbd_lo_done, 4 * st.batch + g + 1)
                    three_passes(ps_c[:, :], [
                        ((vbd_hi[:, g, pair * P:(pair + 1) * P], vbd_lo[:, g, pair * P:(pair + 1) * P]),
                         (pT_hi[:, pair, :], pT_lo[:, pair, :])) for pair in range(PAIRS)]).then_inc(c_product, 1)
                if isinstance(c, int) and c == -1 and g == G - 1:
                    project_values()

            all_steps(pe, slot)

        @block.scalar
        def _(act):
            def to_hi(dst, src):
                return nc.scalar.activation(dst, src, ACT.Copy)

            for g in range(G):
                act.wait_ge(keys_product, g + 1)
                to_hi(keys_hi[:, g, :], ps_k[g][:, :]).then_inc(keys_hi_done, 1)
            for k in range(KT):
                act.wait_ge(wq_loaded[k], 16)
                to_hi(wq_hi[:, k, :], wqo_raw[:, k, :]).then_inc(wq_hi_done, 1)

            def enter_values(batch, c, g):
                wait(act, c_product, 4 * c + g + 1)
                for half in range(2):
                    src = values[64 * half:64 * half + 64, bass.ds(batch, 1), PAIRS * g:PAIRS * (g + 1), :]
                    last = to_hi(value_blocks(vbd_hi, half, g), src.rearrange("p b r d -> p (b r) d"))
                last.then_inc(vbd_hi_done, 1)

            def exponentials(before, gb, u):
                n = 8 * (before.c + 1) + 2 * gb
                if u == 0:
                    wait(act, pT_done, n - 6)
                wait(act, shifted_done, n + u + 1)
                nc.scalar.activation(
                    probs[:, gb, 2 * u:2 * u + 2, :],
                    shifted[:, u, :].rearrange("p (t n) -> p t n", t=2),
                    ACT.Exp, scale=SCALE).then_inc(exp_done, 1)

            def slot(st, g, before, gb):
                c, cb = st.c, before.c
                first = isinstance(c, int) and c == -1
                if before.stage2:
                    if gb == 0:
                        wait(act, o_product, 4 * (cb - 1))
                    wait(act, c_product, 4 * cb + gb + 1)
                    to_hi(c_hi[:, before.odd, gb, :], ps_c[:, :]).then_inc(c_hi_done, 1)
                if st.split:
                    wait(act, xT_loaded[g], 16 * (c + 3))
                    if g == 0:
                        wait(act, q_product, 4 * c + 4)
                    to_hi(x_hi[:, st.odd, g, :], xT_raw[:, g, :]).then_inc(x_hi_done, 1)
                if before.stage1:
                    exponentials(before, gb, 0)
                if st.stage1:
                    n = 4 * (c + 1) + g
                    wait(act, scores_done, 2 * (n - 1))
                    wait(act, q_product, n + 1)
                    to_hi(q_hi[:, g % 2, :], ps_q[g % 2][:, :]).then_inc(q_hi_done, 1)
                if before.stage1:
                    exponentials(before, gb, 1)
                if st.stage2:
                    wait(act, c_product, 4 * c + g)
                    for pair in range(PAIRS):
                        wait(act, pT_done, 8 * c + 2 * g + pair + 1)
                        to_hi(pT_hi[:, pair, :], ps_t[pair][:, :]).then_inc(pT_hi_done, 1)
                if before.output:
                    n = 4 * (cb - 1) + gb
                    s = gb % 2
                    wait(act, shift_done, n + 1)
                    wait(act, y_stored[s], 16 * (2 * (cb - 1) + gb // 2))
                    nc.scalar.activation(y[:, s, :], z[:, s, :], ACT.Identity, bias=shift[:, s:s + 1],
                                         scale=rstd[:, s:s + 1]).then_inc(normed_done, 1)
                if before.next_keys:
                    wait(act, scores_done, 8 * (cb + 1) + 2 * gb + 2)
                    if isinstance(cb, int) and cb == -2 and gb == 0:
                        act.wait_ge(keys_lo_done, G)
                        act.wait_ge(blocks_zeroed, 4)
                    for whole, bd in ((keys_hi, kbd_hi), (keys_lo, kbd_lo)):
                        for j in range(HG):
                            rows = slice(DK * j, DK * j + DK)
                            last = to_hi(bd[rows, gb, KEYS * j:KEYS * (j + 1)],
                                         whole[rows, gb, bass.ds(KEYS * (before.batch + 1), KEYS)].bitcast(fp32))
                    last.then_inc(kbd_done, 1)
                if before.next_values and not (isinstance(cb, int) and cb == -1):
                    enter_values(before.batch, cb, gb)
                if first and g == G - 1:
                    for b2 in range(BATCHES // 2):
                        act.wait_ge(values_product, b2 + 1)
                        for b in range(2):
                            for half in range(2):
                                src = ps_v[b2][KEYS * b:KEYS * (b + 1), :].rearrange(
                                    "p (r h d) -> p r h d", h=2, d=DK)[:, :, half, :]
                                last = nc.scalar.activation(
                                    values[64 * half:64 * half + 64, 2 * b2 + b, :, :], src, ACT.Copy)
                        last.then_inc(values_done, 1)
                    act.wait_ge(values_done, 4)
                    for group in range(G):
                        enter_values(0, c, group)
                    for k in range(KT):
                        act.wait_ge(wo_loaded[k], 16)
                        to_hi(wo_hi[:, k, :], wqo_raw[:, k, :]).then_inc(wo_hi_done, 1)

            all_steps(act, slot)

        @block.vector
        def _(dve):
            def to_lo(dst, whole, hi):
                return nc.vector.tensor_tensor(dst, whole, hi.bitcast(fp32), ALU.subtract)

            for t in (kbd_hi, kbd_lo, vbd_hi, vbd_lo):
                nc.vector.memset(t[:, :, :].bitcast(fp32), 0.0).then_inc(blocks_zeroed, 1)
            for k in range(KT):
                dve.wait_ge(wq_hi_done, k + 1)
                to_lo(wq_lo[:, k, :], wqo_raw[:, k, :], wq_hi[:, k, :]).then_inc(wq_lo_done, 1)
                if k == 0:
                    for g in range(G):
                        dve.wait_ge(keys_hi_done, g + 1)
                        to_lo(keys_lo[:, g, :], ps_k[g][:, :], keys_hi[:, g, :]).then_inc(keys_lo_done, 1)

            def enter_values(batch, g):
                dve.wait_ge(vbd_hi_done, 4 * batch + g + 1)
                for half in range(2):
                    src = values[64 * half:64 * half + 64, bass.ds(batch, 1), PAIRS * g:PAIRS * (g + 1), :]
                    last = to_lo(value_blocks(vbd_lo, half, g), src.rearrange("p b r d -> p (b r) d"),
                                 value_blocks(vbd_hi, half, g))
                last.then_inc(vbd_lo_done, 1)

            def maximum(before, gb, u):
                dve.wait_ge(scores_done, 8 * (before.c + 1) + 2 * gb + u + 1)
                nc.vector.tensor_reduce(row_max[:, u, :], ps_s[u][:, :].rearrange("p (h k) -> p h k", k=KEYS),
                                        axis=AX.X, op=ALU.max).then_inc(max_done, 1)

            def less_maximum(before, gb, u):
                n = 8 * (before.c + 1) + 2 * gb + u
                dve.wait_ge(max_done, n + 1)
                wait(dve, exp_done, n - 1)
                nc.vector.tensor_tensor(
                    shifted[:, u, :].rearrange("p (h k) -> p h k", k=KEYS),
                    ps_s[u][:, :].rearrange("p (h k) -> p h k", k=KEYS),
                    row_max[:, u, :].unsqueeze(2).to_broadcast([P, UH, KEYS]),
                    ALU.subtract).then_inc(shifted_done, 1)

            def exp_sum(before, gb, u):
                dve.wait_ge(exp_done, 8 * (before.c + 1) + 2 * gb + u + 1)
                nc.vector.tensor_reduce(
                    row_sum[:, u, :].rearrange("p (t h) -> p t h", t=2),
                    probs[:, gb, 2 * u:2 * u + 2, :].rearrange("p t (h k) -> p t h k", k=KEYS),
                    axis=AX.X, op=ALU.add).then_inc(sum_done, 1)

            def slot(st, g, before, gb):
                c, cb = st.c, before.c
                first = isinstance(c, int) and c == -1
                if before.stage1:
                    maximum(before, gb, 0)
                if before.output:
                    dve.wait_ge(stats_done, 4 * (cb - 1) + gb + 1)
                if before.stage1:
                    maximum(before, gb, 1)
                if before.output:
                    nc.vector.bn_aggr(mean_var[:, gb % 2, :], stats[:, gb % 2, :]).then_inc(mean_var_done, 1)
                if before.stage1:
                    less_maximum(before, gb, 0)
                    less_maximum(before, gb, 1)
                if before.output:
                    s = gb % 2
                    dve.wait_ge(mean_var_done, 4 * (cb - 1) + gb + 1)
                    nc.vector.tensor_scalar(var_eps[:, s:s + 1], mean_var[:, s, 1:2], EPS, None, ALU.add)
                    nc.vector.tensor_scalar(neg_mean[:, s:s + 1], mean_var[:, s, 0:1], -1.0, None,
                                            ALU.mult).then_inc(moments_done, 1)
                if before.stage2:
                    dve.wait_ge(c_hi_done, 4 * cb + gb + 1)
                    to_lo(c_lo[:, before.odd, gb, :], ps_c[:, :], c_hi[:, before.odd, gb, :]).then_inc(c_lo_done, 1)
                if before.stage1:
                    exp_sum(before, gb, 0)
                if st.stage1:
                    dve.wait_ge(q_hi_done, 4 * (c + 1) + g + 1)
                    to_lo(q_lo[:, g % 2, :], ps_q[g % 2][:, :], q_hi[:, g % 2, :]).then_inc(q_lo_done, 1)
                if before.stage1:
                    exp_sum(before, gb, 1)
                if st.stage2:
                    dve.wait_ge(pT_hi_done, 8 * c + 2 * g + 1)
                    to_lo(pT_lo[:, 0, :], ps_t[0][:, :], pT_hi[:, 0, :]).then_inc(pT_lo_done, 1)
                if before.stage1:
                    n = 8 * (cb + 1) + 2 * gb
                    dve.wait_ge(sum_done, n + 2)
                    wait(dve, probs_done, n)
                    nc.vector.reciprocal(row_inv[:, :, :], row_sum[:, :, :]).then_inc(inv_done, 1)
                if st.stage2:
                    dve.wait_ge(pT_hi_done, 8 * c + 2 * g + 2)
                    to_lo(pT_lo[:, 1, :], ps_t[1][:, :], pT_hi[:, 1, :]).then_inc(pT_lo_done, 1)
                if before.next_values and not (isinstance(cb, int) and cb == -1):
                    enter_values(before.batch, gb)
                if st.output:
                    n = 4 * (c - 1) + g
                    s = g % 2
                    dve.wait_ge(o_product, n + 1)
                    dve.wait_ge(biased_done, n + 1)
                    nc.vector.tensor_tensor(z[:, s, :], ps_o[:, :], z[:, s, :], ALU.add).then_inc(z_done, 1)
                    dve.wait_ge(z_done, n + 1)
                    nc.vector.bn_stats(stats[:, s, :], z[:, s, :]).then_inc(stats_done, 1)
                if first and g == G - 1:
                    for group in range(G):
                        enter_values(0, group)
                    for k in range(KT):
                        dve.wait_ge(wo_hi_done, k + 1)
                        to_lo(wo_lo[:, k, :], wqo_raw[:, k, :], wo_hi[:, k, :]).then_inc(wo_lo_done, 1)

            all_steps(dve, slot)

        @block.gpsimd
        def _(pool):
            nc.gpsimd.memset(minus_half[:, :], -0.5)
            nc.gpsimd.memset(ident[:, :], 0.0).then_inc(ident_zeroed, 1)
            pool.wait_ge(ident_zeroed, 1)
            nc.gpsimd.affine_select(out=ident[:, :], in_=ident[:, :], compare_op=ALU.not_equal, fill=1.0,
                                    base=0, pattern=[[-1, P]], channel_multiplier=1).then_inc(ident_done, 1)
            pool.wait_ge(ident_done, 1)

            def slot(st, g, before, gb):
                c, cb = st.c, before.c
                if st.split:
                    n = 4 * (c + 2) + g
                    pool.wait_ge(x_hi_done, n + 1)
                    nc.gpsimd.tensor_tensor(x_lo[:, st.odd, g, :], xT_raw[:, g, :],
                                            x_hi[:, st.odd, g, :].bitcast(fp32), ALU.subtract
                                            ).then_inc(x_lo_done, 1)
                if before.output:
                    n = 4 * (cb - 1) + gb
                    s = gb % 2
                    pool.wait_ge(moments_done, n + 1)
                    nc.gpsimd.tensor_tensor(rstd[:, s:s + 1], var_eps[:, s:s + 1], minus_half[:, :], ALU.pow
                                            ).then_inc(rstd_done, 1)
                    pool.wait_ge(rstd_done, n + 1)
                    nc.gpsimd.tensor_tensor(shift[:, s:s + 1], neg_mean[:, s:s + 1], rstd[:, s:s + 1], ALU.mult
                                            ).then_inc(shift_done, 1)
                if st.output:
                    n = 4 * (c - 1) + g
                    s = g % 2
                    if isinstance(c, int) and c == 1 and g == 0:
                        pool.wait_ge(rows_loaded, 48)
                    wait(pool, x_loaded[s], 16 * (2 * (c - 1) + g // 2 + 1))
                    wait(pool, normed_done, n - 1)
                    nc.gpsimd.tensor_tensor(z[:, s, :], x_raw[:, s, :], bias_row[:, :], ALU.add
                                            ).then_inc(biased_done, 1)
                if before.stage1:
                    pool.wait_ge(inv_done, 4 * (cb + 1) + gb + 1)
                    for u in range(UNITS):
                        part = probs[:, gb, 2 * u:2 * u + 2, :].rearrange("p t (h k) -> p t h k", k=KEYS)
                        inv = row_inv[:, u, :].rearrange("p (t h) -> p t h", t=2)
                        nc.gpsimd.tensor_tensor(part, part, inv.unsqueeze(3).to_broadcast([P, 2, HG, KEYS]),
                                                ALU.mult).then_inc(probs_done, 1)
                if before.output:
                    n = 4 * (cb - 1) + gb
                    s = gb % 2
                    pool.wait_ge(normed_done, n + 1)
                    nc.gpsimd.tensor_tensor(y[:, s, :], y[:, s, :], gamma_row[:, :], ALU.mult
                                            ).then_inc(scaled_done, 1)
                    pool.wait_ge(scaled_done, n + 1)
                    nc.gpsimd.tensor_tensor(y[:, s, :], y[:, s, :], beta_row[:, :], ALU.add
                                            ).then_inc(y_done, 1)

            all_steps(pool, slot)


def kernel(x, ctx_1024, L0_xattn_w_q, L0_xattn_w_k, L0_xattn_w_v, L0_xattn_w_o, L0_xattn_b_o,
           L0_xattn_ln_gamma, L0_xattn_ln_beta):
    import numpy as np
    import concourse.bacc as bacc
    from concourse.bass_utils import run_bass_kernel_spmd

    x = np.asarray(x)
    rows = x.reshape(-1, x.shape[-1])
    ctx_rows = np.asarray(ctx_1024).reshape(-1, x.shape[-1])
    arrays = {"xT": rows.T, "x": rows, "ctxT": ctx_rows.T,
              "wqT": np.asarray(L0_xattn_w_q).T, "wkT": np.asarray(L0_xattn_w_k).T,
              "wvT": np.asarray(L0_xattn_w_v).T, "woT": np.asarray(L0_xattn_w_o).T,
              "b_o": np.asarray(L0_xattn_b_o), "gamma": np.asarray(L0_xattn_ln_gamma),
              "beta": np.asarray(L0_xattn_ln_beta)}
    arrays = {f"in_{name}": np.ascontiguousarray(a) for name, a in arrays.items()}
    nc = bacc.Bacc("TRN2", target_bir_lowering=False, num_devices=1)
    args = [nc.dram_tensor(name, a.shape, mybir.dt.from_np(a.dtype), kind="ExternalInput").ap()
            for name, a in arrays.items()]
    out = nc.dram_tensor("out", rows.shape, mybir.dt.from_np(rows.dtype), kind="ExternalOutput").ap()
    cross_attention_kernel(nc, *args, out)
    result = run_bass_kernel_spmd(nc, [arrays], core_ids=[0])
    return result.results[0]["out"].reshape(x.shape)
```

```python
from collections import namedtuple
from contextlib import ExitStack

import concourse.bass as bass
from concourse import mybir

Step = namedtuple("Step", "c odd batch split stage1 stage2 output next_keys next_values")


def cross_attention_kernel(nc, xT, x, ctxT, wqT, wkT, wvT, woT, b_o, gamma, beta, out):
    fp32, fp32r = mybir.dt.float32, mybir.dt.float32r
    ALU, ACT, AX = mybir.AluOpType, mybir.ActivationFunctionType, mybir.AxisListType

    P = 128
    DM, ROWS = xT.shape
    CTX_ROWS = ctxT.shape[1]
    BATCHES, HEADS = 8, 16
    KEYS = CTX_ROWS // BATCHES
    DK = DM // HEADS
    KT = DM // P
    CHUNK = 512
    CHUNKS = ROWS // CHUNK
    G = KT
    HG = HEADS // G
    PAIRS = HG // 2
    TH = G * HG
    TILES = CHUNKS * G
    WARM = 20
    LAST = 5
    SCALE = float(DK) ** -0.5
    EPS = 1e-5
    assert CHUNKS == 2 * BATCHES and G == CHUNK // P and 2 * KEYS == P and KT * P == DM

    def step_of(c, odd, batch, whole=False):
        if whole:
            return Step(c, odd, batch, True, True, True, True, not odd, odd)
        return Step(c, odd, batch, 0 <= c + 2 < CHUNKS, 0 <= c + 1 < CHUNKS, 0 <= c < CHUNKS,
                    0 <= c - 1 < CHUNKS, not odd and 0 <= batch + 1 < BATCHES, odd and 0 <= batch < BATCHES)

    def all_steps(eng, slot):
        def quarters(st, last_step):
            for g in range(G):
                slot(st, g, last_step if g == 0 else st, (g - 1) % G)

        def fixed(c):
            return step_of(c, c % 2, (c + 1) // 2)

        for c in range(-2, 3):
            quarters(fixed(c), fixed(c - 1))
        with eng.Fori(1, BATCHES - 2) as i:
            even, odd = step_of(2 * i, 0, i, whole=True), step_of(2 * i + 1, 1, i + 1, whole=True)
            quarters(odd, even)
            quarters(step_of(2 * i + 2, 0, i + 1, whole=True), odd)
        for c in range(CHUNKS - 3, CHUNKS + 1):
            quarters(fixed(c), fixed(c - 1))
        slot(fixed(CHUNKS + 1), 0, fixed(CHUNKS), G - 1)

    def last_tile(st, g):
        return isinstance(st.c, int) and 4 * (st.c - 1) + g >= TILES - LAST

    def transposed_first(st, g):
        return isinstance(st.c, int) and (st.c == 0 or st.c == CHUNKS - 1 and g == 0)

    def wait(eng, sem, value):
        if not isinstance(value, int) or value > 0:
            eng.wait_ge(sem, value)

    xT_v = xT.rearrange("(k p) n -> k p n", p=P)
    ctxT_v, wqT_v, wkT_v, wvT_v, woT_v = (
        a.rearrange("(k p) n -> k p n", p=P) for a in (ctxT, wqT, wkT, wvT, woT))

    with ExitStack() as ctx:
        def sb(name, shape, dt, stack=ctx):
            return stack.enter_context(nc.sbuf_tensor(name, shape, dt))

        def sem(name):
            return ctx.enter_context(nc.semaphore(name))

        def tiled(names, dt, stack=ctx):
            return [sb(name, [P, KT, DM], dt, stack) for name in names]

        with ExitStack() as raw:
            wq_raw, wo_raw, wv_raw = tiled(("wq_raw", "wo_raw", "wv_raw"), fp32, raw)
        wq_lo, wo_lo, wv_lo = tiled(("wq_lo", "wo_lo", "wv_lo"), fp32r)
        wq_hi, wo_hi = tiled(("wq_hi", "wo_hi"), fp32r)
        keys_hi, keys_lo = sb("keys_hi", [P, G, CTX_ROWS], fp32r), sb("keys_lo", [P, G, CTX_ROWS], fp32r)
        values = sb("values", [P, BATCHES, HEADS // 2, DK], fp32)
        kbd_hi, kbd_lo = sb("kbd_hi", [P, G, HG * KEYS], fp32r), sb("kbd_lo", [P, G, HG * KEYS], fp32r)
        vbd_hi, vbd_lo = sb("vbd_hi", [P, G, PAIRS * P], fp32r), sb("vbd_lo", [P, G, PAIRS * P], fp32r)
        bias_row, gamma_row, beta_row = (sb(n, [P, DM], fp32) for n in ("bias_row", "gamma_row", "beta_row"))
        ident = sb("ident", [P, P], fp32)
        minus_half = sb("minus_half", [P, 1], fp32)
        xT_raw = sb("xT_raw", [P, KT, CHUNK], fp32)
        x_hi, x_lo = sb("x_hi", [P, 2, KT, CHUNK], fp32r), sb("x_lo", [P, 2, KT, CHUNK], fp32r)
        q_hi, q_lo = sb("q_hi", [P, 2, CHUNK], fp32r), sb("q_lo", [P, 2, CHUNK], fp32r)
        shifted = sb("shifted", [P, TH, KEYS], fp32)
        row_max, row_sum, row_inv = (sb(n, [P, TH], fp32) for n in ("row_max", "row_sum", "row_inv"))
        pT_hi, pT_lo = sb("pT_hi", [P, PAIRS, CHUNK], fp32r), sb("pT_lo", [P, PAIRS, CHUNK], fp32r)
        x_raw = sb("x_raw", [P, 2, DM], fp32)
        stats = sb("stats", [P, 2, 6], fp32)
        mean_var = sb("mean_var", [P, 2, 2], fp32)
        neg_mean, var_eps, rstd, shift = (sb(n, [P, 2], fp32) for n in ("neg_mean", "var_eps", "rstd", "shift"))
        with ExitStack() as raw:
            wk_raw, _, ctx_raw = tiled(("wk_raw", "wk_hi_place", "ctx_raw"), fp32, raw)
        with ExitStack() as first:
            wk_lo, wk_hi, ctx_lo, ctx_hi, wv_hi = tiled(("wk_lo", "wk_hi", "ctx_lo", "ctx_hi", "wv_hi"), fp32r, first)
        c_hi, c_lo = [None, None], [None, None]
        for odd in range(2):
            c_hi[odd] = sb(f"c_hi{odd}", [P, G, CHUNK], fp32r)
            c_lo[odd] = sb(f"c_lo{odd}", [P, G, CHUNK], fp32r)
        z = sb("z", [P, 2, DM], fp32)
        y = sb("y", [P, 2, DM], fp32)
        probs = sb("probs", [P, G, G, HG * KEYS], fp32)

        def ps(name, banks):
            return ctx.enter_context(nc.psum_tensor(name, [P, banks, 512], fp32))

        ps_q, ps_s, ps_t, ps_c, ps_o = ps("ps_q", 2), ps("ps_s", 2), ps("ps_t", 2), ps("ps_c", 1), ps("ps_o", 1)
        ps_k = [ps_q[:, 0, :], ps_q[:, 1, :], ps_s[:, 0, :], ps_s[:, 1, :]]
        ps_v = [ps_t[:, 0, :], ps_t[:, 1, :], ps_o[:, 0, :], ps_o[:, 0, :]]

        def output_bank(c, g):
            return ps_q[:, 0, :] if isinstance(c, int) and c >= CHUNKS - 1 and g % 2 else ps_o[:, 0, :]

        ctx_loaded, wk_loaded, wv_loaded, wq_loaded, wo_loaded = (
            [sem(f"{n}_loaded{k}") for k in range(KT)] for n in ("ctx", "wk", "wv", "wq", "wo"))
        rows_loaded = sem("rows_loaded")
        xT_loaded = [sem(f"xT_loaded{k}") for k in range(KT)]
        x_loaded = [sem(f"x_loaded{s}") for s in range(2)]
        y_stored = [sem(f"y_stored{s}") for s in range(2)]
        blocks_zeroed, ident_zeroed, ident_done = sem("blocks_zeroed"), sem("ident_zeroed"), sem("ident_done")
        keys_product, keys_hi_done, keys_lo_done = sem("keys_product"), sem("keys_hi_done"), sem("keys_lo_done")
        values_product, values_done = sem("values_product"), sem("values_done")
        ctx_hi_done, wk_hi_done, wq_hi_done, wv_hi_done, wo_hi_done = (
            sem(f"{n}_hi_done") for n in ("ctx", "wk", "wq", "wv", "wo"))
        ctx_lo_done, wk_lo_done, wq_lo_done, wv_lo_done, wo_lo_done = (
            sem(f"{n}_lo_done") for n in ("ctx", "wk", "wq", "wv", "wo"))
        x_hi_done, x_lo_done = sem("x_hi_done"), sem("x_lo_done")
        q_product, q_hi_done, q_lo_done = sem("q_product"), sem("q_hi_done"), sem("q_lo_done")
        kbd_done, vbd_hi_done, vbd_lo_done = sem("kbd_done"), sem("vbd_hi_done"), sem("vbd_lo_done")
        scores_done, max_done, shifted_done, exp_done = (
            sem(n) for n in ("scores_done", "max_done", "shifted_done", "exp_done"))
        sum_done, inv_done, probs_done = sem("sum_done"), sem("inv_done"), sem("probs_done")
        pT_done, pT_hi_done, pT_lo_done = sem("pT_done"), sem("pT_hi_done"), sem("pT_lo_done")
        c_product, c_hi_done, c_lo_done = sem("c_product"), sem("c_hi_done"), sem("c_lo_done")
        o_product, biased_done, z_done = sem("o_product"), sem("biased_done"), sem("z_done")
        stats_done, mean_var_done, moments_done = sem("stats_done"), sem("mean_var_done"), sem("moments_done")
        rstd_done, shift_done, normed_done, scaled_done, y_done = (
            sem(n) for n in ("rstd_done", "shift_done", "normed_done", "scaled_done", "y_done"))

        last_scaled_done, last_y_done = sem("last_scaled_done"), sem("last_y_done")

        def value_blocks(t, half, g):
            return t[64 * half:64 * half + 64, g, :].rearrange("p (x c) -> p x c", c=64)[
                :, 0:4:3, DK * half:DK * half + DK]

        block = ctx.enter_context(nc.Block())

        @block.sync
        def _(sp):
            def load(raw, k, src, loaded):
                sp.dma_start(raw[:, k, :], src[k, :, :]).then_inc(loaded[k], 16)

            for k in range(KT):
                load(ctx_raw, k, ctxT_v, ctx_loaded)
                load(wk_raw, k, wkT_v, wk_loaded)
            for k in range(KT):
                load(wq_raw, k, wqT_v, wq_loaded)
            for k in range(KT):
                sp.dma_start(xT_raw[:, k, :], xT_v[k, :, 0:CHUNK]).then_inc(xT_loaded[k], 16)
            for k in range(KT):
                load(wv_raw, k, wvT_v, wv_loaded)

            def slot(st, g, before, gb):
                c = st.c
                tile = 4 * (c - 1) + g
                if isinstance(c, int) and c == -1 and g == 0:
                    for k in range(KT):
                        load(wo_raw, k, woT_v, wo_loaded)
                    for row, src in ((bias_row, b_o), (gamma_row, gamma), (beta_row, beta)):
                        sp.dma_start(row[:, :], src.partition_broadcast(P)).then_inc(rows_loaded, 16)
                    for s in range(2):
                        sp.dma_start(x_raw[:, s, :], x[s * P:(s + 1) * P, :]).then_inc(x_loaded[s], 16)
                if (st.output or before.output) and (not isinstance(c, int) or 1 < tile < TILES - LAST + 2):
                    wait(sp, y_done, tile - 1)
                    sp.dma_start(out[bass.ds(P * (tile - 2), P), :], y[:, g % 2, :]).then_inc(y_stored[g % 2], 16)
                if st.output and (not isinstance(c, int) or tile + 2 < TILES):
                    wait(sp, biased_done, tile + 1)
                    sp.dma_start(x_raw[:, g % 2, :], x[bass.ds(P * (tile + 2), P), :]
                                 ).then_inc(x_loaded[g % 2], 16)
                if st.split and (not isinstance(c, int) or c + 3 < CHUNKS):
                    wait(sp, x_lo_done, 4 * (c + 2) + g + 1)
                    sp.dma_start(xT_raw[:, g, :], xT_v[g, :, bass.ds(CHUNK * (c + 3), CHUNK)]
                                 ).then_inc(xT_loaded[g], 16)

            all_steps(sp, slot)
            for n in range(LAST):
                sp.wait_ge(last_y_done, n + 1)
                tile = TILES - LAST + n
                sp.dma_start(out[P * tile:P * (tile + 1), :], y[:, tile % 2, :]).then_inc(y_stored[tile % 2], 16)
            for s in range(2):
                sp.wait_ge(y_stored[s], 16 * TILES // 2)

        @block.tensor
        def _(pe):
            def three_passes(dst, pairs, first=True, last=True):
                passes = [p for (l_hi, l_lo), (r_hi, r_lo) in pairs
                          for p in ((l_lo, r_hi), (l_hi, r_lo), (l_hi, r_hi))]
                for n, (lhs, rhs) in enumerate(passes):
                    mm = nc.tensor.matmul(dst, lhs, rhs, start=(first and n == 0),
                                          stop=(last and n == len(passes) - 1))
                return mm

            pe.wait_ge(ident_done, 1)
            for _ in range(WARM):
                nc.tensor.transpose(ps_t[:, 0, 0:P], ident[:, :], ident[:, :])

            for k in range(KT):
                pe.wait_ge(ctx_lo_done, k + 1)
                pe.wait_ge(wk_lo_done, k + 1)
                for g in range(G):
                    dims = slice(g * P, (g + 1) * P)
                    mm = three_passes(ps_k[g], [((wk_hi[:, k, dims], wk_lo[:, k, dims]),
                                                 (ctx_hi[:, k, :], ctx_lo[:, k, :]))],
                                      first=(k == 0), last=(k == KT - 1))
                    if k == KT - 1:
                        mm.then_inc(keys_product, 1)

            def project_values(first, count):
                for b2, k in (divmod(n, KT) for n in range(first, first + count)):
                    if b2 == 3 and k == 0:
                        pe.wait_ge(values_done, 3)
                    pe.wait_ge(wv_lo_done, k + 1)
                    keys = slice(b2 * P, (b2 + 1) * P)
                    mm = three_passes(ps_v[b2], [((ctx_hi[:, k, keys], ctx_lo[:, k, keys]),
                                                  (wv_hi[:, k, :], wv_lo[:, k, :]))],
                                      first=(k == 0), last=(k == KT - 1))
                    if k == KT - 1:
                        mm.then_inc(values_product, 1)

            def slot(st, g, before, gb):
                c = st.c
                if st.stage1:
                    n = 4 * (c + 1) + g
                    par = 1 - st.odd
                    if isinstance(c, int) and c == -1:
                        pe.wait_ge(keys_lo_done, g + 1)
                    elif g == 0:
                        wait(pe, x_lo_done, n + 4)
                    wait(pe, q_lo_done, n - 1)
                    for k in range(KT):
                        if isinstance(c, int) and c == -1 and g == 0:
                            pe.wait_ge(x_lo_done, k + 1)
                            pe.wait_ge(wq_lo_done, k + 1)
                        mm = three_passes(ps_q[:, g % 2, :], [
                            ((wq_hi[:, k, g * P:(g + 1) * P], wq_lo[:, k, g * P:(g + 1) * P]),
                             (x_hi[:, par, k, :], x_lo[:, par, k, :]))], first=(k == 0), last=(k == KT - 1))
                    mm.then_inc(q_product, 1)
                if isinstance(c, int) and c == -1:
                    project_values(*((0, 2), (2, 3), (5, 3), (8, 4))[g])
                if st.stage2:
                    n = 4 * c + g
                    wait(pe, probs_done, n + 1)
                    wait(pe, pT_lo_done, n)
                    if isinstance(c, int) and c == 0 and g == 0:
                        pe.wait_ge(values_done, 2)
                    for pair in range(PAIRS):
                        for t in range(G):
                            mm = nc.tensor.transpose(ps_t[:, pair, t * P:(t + 1) * P],
                                                     probs[:, g, t, pair * P:(pair + 1) * P], ident[:, :])
                    mm.then_inc(pT_done, 1)
                if isinstance(c, int) and c == 0:
                    project_values(12 + g, 1)
                if st.output:
                    n = 4 * (c - 1) + g
                    par = 1 - st.odd
                    if g == 0:
                        wait(pe, c_lo_done, n + 3)
                        if isinstance(c, int) and c == 1:
                            pe.wait_ge(wo_lo_done, KT)
                    if isinstance(c, int) and c == 1 and g == 0:
                        pe.wait_ge(values_done, 4)
                    if isinstance(c, int) and c >= CHUNKS - 1 and (c, g) != (CHUNKS - 1, 0):
                        pe.wait_ge(z_done, n - 1)
                        pe.wait_ge(q_lo_done, 4 * CHUNKS)
                    else:
                        wait(pe, z_done, n)
                    groups = [((c_hi[par][:, k, g * P:(g + 1) * P], c_lo[par][:, k, g * P:(g + 1) * P]),
                               (wo_hi[:, k, :], wo_lo[:, k, :])) for k in range(KT)]
                    three_passes(output_bank(c, g), groups[:-1], last=False)
                    if g == 0:
                        wait(pe, c_lo_done, n + 4)
                    three_passes(output_bank(c, g), groups[-1:], first=False).then_inc(o_product, 1)
                if st.stage1:
                    n = 4 * (c + 1) + g
                    wait(pe, q_lo_done, n + 1)
                    if st.odd:
                        wait(pe, kbd_done, 4 * st.batch + g + 1)
                    wait(pe, shifted_done, n)
                    for t in range(G):
                        rows = slice(t * P, (t + 1) * P)
                        mm = three_passes(ps_s[:, t // 2, (t % 2) * HG * KEYS:(t % 2 + 1) * HG * KEYS], [
                            ((q_hi[:, g % 2, rows], q_lo[:, g % 2, rows]),
                             (kbd_hi[:, g, :], kbd_lo[:, g, :]))])
                    mm.then_inc(scores_done, 1)
                if st.stage2:
                    n = 4 * c + g
                    wait(pe, pT_lo_done, n + 1)
                    wait(pe, c_lo_done, n)
                    if not st.odd:
                        wait(pe, vbd_lo_done, 4 * st.batch + g + 1)
                    three_passes(ps_c[:, 0, :], [
                        ((vbd_hi[:, g, pair * P:(pair + 1) * P], vbd_lo[:, g, pair * P:(pair + 1) * P]),
                         (pT_hi[:, pair, :], pT_lo[:, pair, :])) for pair in range(PAIRS)]).then_inc(c_product, 1)

            all_steps(pe, slot)

        @block.scalar
        def _(act):
            def to_hi(dst, src):
                return nc.scalar.activation(dst, src, ACT.Copy)

            def split_hi(hi, raw, k, loaded, done):
                act.wait_ge(loaded[k], 16)
                to_hi(hi[:, k, :], raw[:, k, :]).then_inc(done, 1)

            for k in range(KT):
                split_hi(ctx_hi, ctx_raw, k, ctx_loaded, ctx_hi_done)
                split_hi(wk_hi, wk_raw, k, wk_loaded, wk_hi_done)
            for k in range(KT):
                split_hi(wq_hi, wq_raw, k, wq_loaded, wq_hi_done)

            def split_x(st, g):
                c = st.c
                wait(act, xT_loaded[g], 16 * (c + 3))
                if g == 0:
                    wait(act, q_product, 4 * c + 4)
                to_hi(x_hi[:, st.odd, g, :], xT_raw[:, g, :]).then_inc(x_hi_done, 1)

            def enter_keys(batch, g):
                for whole, bd in ((keys_hi, kbd_hi), (keys_lo, kbd_lo)):
                    for j in range(HG):
                        rows = slice(DK * j, DK * j + DK)
                        last = to_hi(bd[rows, g, KEYS * j:KEYS * (j + 1)],
                                     whole[rows, g, bass.ds(KEYS * batch, KEYS)].bitcast(fp32))
                last.then_inc(kbd_done, 1)

            def enter_values(batch, c, g):
                wait(act, c_product, 4 * c + g + 1)
                if isinstance(c, int) and c == -1:
                    act.wait_ge(values_done, 1)
                for half in range(2):
                    src = values[64 * half:64 * half + 64, bass.ds(batch, 1), PAIRS * g:PAIRS * (g + 1), :]
                    last = to_hi(value_blocks(vbd_hi, half, g), src.rearrange("p b r d -> p (b r) d"))
                last.then_inc(vbd_hi_done, 1)

            def exponentials(c, g):
                n = 4 * (c + 1) + g
                wait(act, pT_done, n - 3)
                wait(act, shifted_done, n + 1)
                nc.scalar.activation(probs[:, g, :, :].rearrange("p t (h k) -> p (t h) k", k=KEYS),
                                     shifted[:, :, :], ACT.Exp, scale=SCALE).then_inc(exp_done, 1)

            def slot(st, g, before, gb):
                c, cb = st.c, before.c
                if before.stage2:
                    if gb == 0:
                        wait(act, o_product, 4 * (cb - 1))
                    wait(act, c_product, 4 * cb + gb + 1)
                    to_hi(c_hi[before.odd][:, gb, :], ps_c[:, 0, :]).then_inc(c_hi_done, 1)
                filling = isinstance(c, int) and c == -1
                if st.split and not filling:
                    split_x(st, g)
                if filling and g == 0:
                    for n in range(G):
                        act.wait_ge(keys_product, n + 1)
                        to_hi(keys_hi[:, n, :], ps_k[n]).then_inc(keys_hi_done, 1)
                    for k in range(2):
                        split_hi(wv_hi, wv_raw, k, wv_loaded, wv_hi_done)
                if filling:
                    act.wait_ge(keys_lo_done, g + 1)
                    act.wait_ge(blocks_zeroed, 4)
                    enter_keys(0, g)
                if st.stage1:
                    n = 4 * (c + 1) + g
                    wait(act, scores_done, n - 1)
                    wait(act, q_product, n + 1)
                    to_hi(q_hi[:, g % 2, :], ps_q[:, g % 2, :]).then_inc(q_hi_done, 1)
                if filling:
                    if g == 0:
                        for k in range(2, KT):
                            split_hi(wv_hi, wv_raw, k, wv_loaded, wv_hi_done)
                    split_x(st, g)
                if before.stage1 and not transposed_first(st, g):
                    exponentials(cb, gb)
                if st.stage2:
                    wait(act, c_product, 4 * c + g)
                    wait(act, pT_done, 4 * c + g + 1)
                    to_hi(pT_hi[:, :, :], ps_t[:, :, :]).then_inc(pT_hi_done, 1)
                if before.stage1 and transposed_first(st, g):
                    exponentials(cb, gb)
                if before.output and not last_tile(before, gb):
                    n = 4 * (cb - 1) + gb
                    s = gb % 2
                    wait(act, shift_done, n + 1)
                    wait(act, y_stored[s], 16 * (2 * (cb - 1) + gb // 2))
                    nc.scalar.activation(y[:, s, :], z[:, s, :], ACT.Identity, bias=shift[:, s:s + 1],
                                         scale=rstd[:, s:s + 1]).then_inc(normed_done, 1)
                if before.next_keys and not (isinstance(cb, int) and cb == -2):
                    wait(act, scores_done, 4 * (cb + 1) + gb + 1)
                    enter_keys(before.batch + 1, gb)
                if isinstance(c, int) and (c == -1 and g > 0 or c == 0 and g == G - 1):
                    b2 = g - 1 if c == -1 else 3
                    act.wait_ge(values_product, b2 + 1)
                    for b in range(2):
                        for half in range(2):
                            src = ps_v[b2][KEYS * b:KEYS * (b + 1), :].rearrange(
                                "p (r h d) -> p r h d", h=2, d=DK)[:, :, half, :]
                            last = nc.scalar.activation(
                                values[64 * half:64 * half + 64, 2 * b2 + b, :, :], src, ACT.Copy)
                    last.then_inc(values_done, 1)
                if before.next_values:
                    enter_values(before.batch, cb, gb)
                if isinstance(c, int) and c == 0:
                    split_hi(wo_hi, wo_raw, g, wo_loaded, wo_hi_done)

            all_steps(act, slot)

        @block.vector
        def _(dve):
            def to_lo(dst, whole, hi):
                return nc.vector.tensor_tensor(dst, whole, hi.bitcast(fp32), ALU.subtract)

            scores = ps_s[:, :, :].rearrange("p b (r k) -> p (b r) k", k=KEYS)

            for t in (kbd_hi, kbd_lo, vbd_hi, vbd_lo):
                nc.vector.memset(t[:, :, :].bitcast(fp32), 0.0).then_inc(blocks_zeroed, 1)

            def split_lo(raw, hi, lo, k, hi_done, lo_done):
                dve.wait_ge(hi_done, k + 1)
                to_lo(lo[:, k, :], raw[:, k, :], hi[:, k, :]).then_inc(lo_done, 1)

            for k in range(KT):
                split_lo(ctx_raw, ctx_hi, ctx_lo, k, ctx_hi_done, ctx_lo_done)
                split_lo(wk_raw, wk_hi, wk_lo, k, wk_hi_done, wk_lo_done)
            for k in range(KT):
                split_lo(wq_raw, wq_hi, wq_lo, k, wq_hi_done, wq_lo_done)

            def enter_values(batch, g):
                dve.wait_ge(vbd_hi_done, 4 * batch + g + 1)
                for half in range(2):
                    src = values[64 * half:64 * half + 64, bass.ds(batch, 1), PAIRS * g:PAIRS * (g + 1), :]
                    last = to_lo(value_blocks(vbd_lo, half, g), src.rearrange("p b r d -> p (b r) d"),
                                 value_blocks(vbd_hi, half, g))
                last.then_inc(vbd_lo_done, 1)

            def sums(c, g):
                dve.wait_ge(exp_done, 4 * (c + 1) + g + 1)
                nc.vector.tensor_reduce(row_sum[:, :], probs[:, g, :, :].rearrange(
                    "p t (h k) -> p (t h) k", k=KEYS), axis=AX.X, op=ALU.add).then_inc(sum_done, 1)

            def slot(st, g, before, gb):
                c, cb = st.c, before.c
                first = isinstance(c, int) and c == -1 and g == 0
                if first:
                    for n in range(G):
                        dve.wait_ge(keys_hi_done, n + 1)
                        to_lo(keys_lo[:, n, :], ps_k[n], keys_hi[:, n, :]).then_inc(keys_lo_done, 1)
                    for k in range(2):
                        split_lo(wv_raw, wv_hi, wv_lo, k, wv_hi_done, wv_lo_done)
                if before.output:
                    dve.wait_ge(stats_done, 4 * (cb - 1) + gb + 1)
                if before.stage1:
                    dve.wait_ge(scores_done, 4 * (cb + 1) + gb + 1)
                    nc.vector.tensor_reduce(row_max[:, :], scores, axis=AX.X, op=ALU.max).then_inc(max_done, 1)
                if before.output:
                    nc.vector.bn_aggr(mean_var[:, gb % 2, :], stats[:, gb % 2, :]).then_inc(mean_var_done, 1)
                if before.stage1:
                    n = 4 * (cb + 1) + gb
                    dve.wait_ge(max_done, n + 1)
                    wait(dve, exp_done, n)
                    nc.vector.tensor_tensor(shifted[:, :, :], scores,
                                            row_max[:, :].unsqueeze(2).to_broadcast([P, TH, KEYS]),
                                            ALU.subtract).then_inc(shifted_done, 1)
                if before.output:
                    s = gb % 2
                    dve.wait_ge(mean_var_done, 4 * (cb - 1) + gb + 1)
                    nc.vector.tensor_scalar(var_eps[:, s:s + 1], mean_var[:, s, 1:2], EPS, None, ALU.add)
                    nc.vector.tensor_scalar(neg_mean[:, s:s + 1], mean_var[:, s, 0:1], -1.0, None,
                                            ALU.mult).then_inc(moments_done, 1)
                if last_tile(before, gb):
                    s = gb % 2
                    n = 4 * (cb - 1) + gb - (TILES - LAST)
                    dve.wait_ge(y_stored[s], 16 * ((TILES - LAST + n) // 2))
                    nc.vector.scalar_tensor_tensor(out=y[:, s, :], in0=z[:, s, :], scalar=mean_var[:, s, 0:1],
                                                   in1=gamma_row[:, :], op0=ALU.subtract, op1=ALU.mult
                                                   ).then_inc(last_scaled_done, 1)
                if before.stage2:
                    dve.wait_ge(c_hi_done, 4 * cb + gb + 1)
                    to_lo(c_lo[before.odd][:, gb, :], ps_c[:, 0, :], c_hi[before.odd][:, gb, :]
                          ).then_inc(c_lo_done, 1)
                if st.stage1:
                    dve.wait_ge(q_hi_done, 4 * (c + 1) + g + 1)
                    to_lo(q_lo[:, g % 2, :], ps_q[:, g % 2, :], q_hi[:, g % 2, :]).then_inc(q_lo_done, 1)
                if first:
                    for k in range(2, KT):
                        split_lo(wv_raw, wv_hi, wv_lo, k, wv_hi_done, wv_lo_done)
                if before.stage1 and not transposed_first(st, g):
                    sums(cb, gb)
                if st.stage2:
                    dve.wait_ge(pT_hi_done, 4 * c + g + 1)
                    to_lo(pT_lo[:, :, :], ps_t[:, :, :], pT_hi[:, :, :]).then_inc(pT_lo_done, 1)
                if before.stage1 and transposed_first(st, g):
                    sums(cb, gb)
                if before.stage1:
                    n = 4 * (cb + 1) + gb
                    dve.wait_ge(sum_done, n + 1)
                    wait(dve, probs_done, n)
                    nc.vector.reciprocal(row_inv[:, :], row_sum[:, :]).then_inc(inv_done, 1)
                if before.next_values:
                    enter_values(before.batch, gb)
                if st.output:
                    n = 4 * (c - 1) + g
                    s = g % 2
                    dve.wait_ge(o_product, n + 1)
                    dve.wait_ge(biased_done, n + 1)
                    nc.vector.tensor_tensor(z[:, s, :], output_bank(c, g), z[:, s, :], ALU.add).then_inc(z_done, 1)
                    dve.wait_ge(z_done, n + 1)
                    nc.vector.bn_stats(stats[:, s, :], z[:, s, :]).then_inc(stats_done, 1)
                if last_tile(before, gb):
                    s = gb % 2
                    n = 4 * (cb - 1) + gb - (TILES - LAST)
                    dve.wait_ge(last_scaled_done, n + 1)
                    dve.wait_ge(rstd_done, TILES - LAST + n + 1)
                    nc.vector.scalar_tensor_tensor(out=y[:, s, :], in0=y[:, s, :], scalar=rstd[:, s:s + 1],
                                                   in1=beta_row[:, :], op0=ALU.mult, op1=ALU.add
                                                   ).then_inc(last_y_done, 1)

            all_steps(dve, slot)

        @block.gpsimd
        def _(pool):
            nc.gpsimd.memset(minus_half[:, :], -0.5)
            nc.gpsimd.memset(ident[:, :], 0.0).then_inc(ident_zeroed, 1)
            pool.wait_ge(ident_zeroed, 1)
            nc.gpsimd.affine_select(out=ident[:, :], in_=ident[:, :], compare_op=ALU.not_equal, fill=1.0,
                                    base=0, pattern=[[-1, P]], channel_multiplier=1).then_inc(ident_done, 1)
            pool.wait_ge(ident_done, 1)

            def add_bias(c, g):
                n = 4 * (c - 1) + g
                s = g % 2
                if isinstance(c, int) and c == 1 and g == 0:
                    pool.wait_ge(rows_loaded, 48)
                    pool.wait_ge(values_product, 4)
                wait(pool, x_loaded[s], 16 * (2 * (c - 1) + g // 2 + 1))
                if isinstance(c, int) and n - 2 >= TILES - LAST:
                    pool.wait_ge(last_scaled_done, n - 1 - (TILES - LAST))
                else:
                    wait(pool, normed_done, n - 1)
                nc.gpsimd.tensor_tensor(z[:, s, :], x_raw[:, s, :], bias_row[:, :], ALU.add
                                        ).then_inc(biased_done, 1)

            def slot(st, g, before, gb):
                c, cb = st.c, before.c
                in_last_step = isinstance(c, int) and c == CHUNKS
                if in_last_step and g != 1:
                    add_bias(c, g)
                if st.split:
                    n = 4 * (c + 2) + g
                    pool.wait_ge(x_hi_done, n + 1)
                    nc.gpsimd.tensor_tensor(x_lo[:, st.odd, g, :], xT_raw[:, g, :],
                                            x_hi[:, st.odd, g, :].bitcast(fp32), ALU.subtract
                                            ).then_inc(x_lo_done, 1)
                if before.output:
                    n = 4 * (cb - 1) + gb
                    s = gb % 2
                    pool.wait_ge(moments_done, n + 1)
                    nc.gpsimd.tensor_tensor(rstd[:, s:s + 1], var_eps[:, s:s + 1], minus_half[:, :], ALU.pow
                                            ).then_inc(rstd_done, 1)
                    if not last_tile(before, gb):
                        pool.wait_ge(rstd_done, n + 1)
                        nc.gpsimd.tensor_tensor(shift[:, s:s + 1], neg_mean[:, s:s + 1], rstd[:, s:s + 1],
                                                ALU.mult).then_inc(shift_done, 1)
                if st.output and not in_last_step:
                    add_bias(c, g)
                if in_last_step and g == 0:
                    add_bias(c, 1)
                if before.stage1:
                    pool.wait_ge(inv_done, 4 * (cb + 1) + gb + 1)
                    part = probs[:, gb, :, :].rearrange("p t (h k) -> p (t h) k", k=KEYS)
                    nc.gpsimd.tensor_tensor(part, part, row_inv[:, :].unsqueeze(2).to_broadcast([P, TH, KEYS]),
                                            ALU.mult).then_inc(probs_done, 1)
                if before.output and not last_tile(before, gb):
                    n = 4 * (cb - 1) + gb
                    s = gb % 2
                    pool.wait_ge(normed_done, n + 1)
                    nc.gpsimd.tensor_tensor(y[:, s, :], y[:, s, :], gamma_row[:, :], ALU.mult
                                            ).then_inc(scaled_done, 1)
                    pool.wait_ge(scaled_done, n + 1)
                    nc.gpsimd.tensor_tensor(y[:, s, :], y[:, s, :], beta_row[:, :], ALU.add
                                            ).then_inc(y_done, 1)

                if isinstance(c, int) and c == 0:
                    pool.wait_ge(wo_hi_done, g + 1)
                    nc.gpsimd.tensor_tensor(wo_lo[:, g, :], wo_raw[:, g, :], wo_hi[:, g, :].bitcast(fp32),
                                            ALU.subtract).then_inc(wo_lo_done, 1)

            all_steps(pool, slot)


def kernel(x, ctx_1024, L0_xattn_w_q, L0_xattn_w_k, L0_xattn_w_v, L0_xattn_w_o, L0_xattn_b_o,
           L0_xattn_ln_gamma, L0_xattn_ln_beta):
    import numpy as np
    import concourse.bacc as bacc
    from concourse.bass_utils import run_bass_kernel_spmd

    x = np.asarray(x)
    rows = x.reshape(-1, x.shape[-1])
    ctx_rows = np.asarray(ctx_1024).reshape(-1, x.shape[-1])
    arrays = {"xT": rows.T, "x": rows, "ctxT": ctx_rows.T,
              "wqT": np.asarray(L0_xattn_w_q).T, "wkT": np.asarray(L0_xattn_w_k).T,
              "wvT": np.asarray(L0_xattn_w_v).T, "woT": np.asarray(L0_xattn_w_o).T,
              "b_o": np.asarray(L0_xattn_b_o), "gamma": np.asarray(L0_xattn_ln_gamma),
              "beta": np.asarray(L0_xattn_ln_beta)}
    arrays = {f"in_{name}": np.ascontiguousarray(a) for name, a in arrays.items()}
    nc = bacc.Bacc("TRN2", target_bir_lowering=False, num_devices=1)
    args = [nc.dram_tensor(name, a.shape, mybir.dt.from_np(a.dtype), kind="ExternalInput").ap()
            for name, a in arrays.items()]
    out = nc.dram_tensor("out", rows.shape, mybir.dt.from_np(rows.dtype), kind="ExternalOutput").ap()
    cross_attention_kernel(nc, *args, out)
    result = run_bass_kernel_spmd(nc, [arrays], core_ids=[0])
    return result.results[0]["out"].reshape(x.shape)
```
